# Optimizing a Trainium2 kernel written in Bass

```python
import numpy as np
import jax
import jax.numpy as jnp

def _softmax(x, axis=-1):
    return jax.nn.softmax(x, axis=axis)

def _gelu(x):
    return jax.nn.gelu(x, approximate=True)

def _silu(x):
    return jax.nn.silu(x)

def _sigmoid(x):
    return jax.nn.sigmoid(x)

def _layernorm(x, axis=-1, eps=1e-05):
    m = jnp.mean(x, axis=axis, keepdims=True)
    v = jnp.var(x, axis=axis, keepdims=True)
    return (x - m) / jnp.sqrt(v + eps)

def _scatter_add(tgt, idx, src, axis=0):
    return tgt.at[idx].add(src)

def _segment_sum(src, seg, n):
    return jax.ops.segment_sum(src, seg, n)
kernel_name = 'mk_gnn_preln_d1_gnn_r64_b369c9'

def setup_inputs(seed: int=0):
    np.random.seed(seed)
    _w = jnp.asarray

    def _rec_inputs():
        import jax
        import jax.numpy as jnp
        _gk = jax.random.key(seed)
        x = -2.321e-05 + 0.0625 * jax.random.normal(jax.random.fold_in(_gk, 1), (50000, 256), jnp.float32)
        src = jax.random.randint(jax.random.fold_in(_gk, 2), (12500,), 0, 50000, jnp.int32)
        dst = jnp.minimum((50000 * jax.random.uniform(jax.random.fold_in(_gk, 3), (12500,)) ** 2.0).astype(jnp.int32), 49999)
        _o = jnp.argsort(dst, stable=True)
        src = src[_o]
        dst = dst[_o]
        edge_type_240 = jax.random.randint(jax.random.fold_in(_gk, 12), (12500,), 0, 240, jnp.int32)
        edge_weight = jax.random.uniform(jax.random.fold_in(_gk, 13), (12500,), jnp.float32, 0.0, 0.999994)
        return (x, src, dst, edge_type_240, edge_weight)
    x, src, dst, edge_type_240, edge_weight = _rec_inputs()

    def _L0_gnn_setup():
        import jax, jax.numpy as jnp
        import numpy as np
        N = 50000
        R = 240
        D = 256
        B = 10
        E = 5000
        RATE = 0.1
        LN_EPS = 1e-05

        def _time_decay(etimes, current_time):
            td = jnp.maximum(current_time - etimes, 0.0)
            td = td / (td.max() + 1e-08)
            return jnp.exp(-RATE * td)[:, None]

        def _rgcn_layer(h, basis, comp, loop_w, bias, src, dst, etypes, enorm):
            hsrc = h[src]
            coef = comp[etypes]
            msg = jnp.zeros_like(hsrc)
            for b in range(basis.shape[0]):
                msg = msg + coef[:, b:b + 1] * (hsrc @ basis[b])
            msg = msg * enorm
            agg = jax.ops.segment_sum(msg, dst, num_segments=h.shape[0])
            return agg + bias + h @ loop_w
        key = jax.random.key(seed)
        ks = jax.random.split(key, 16)
        s = 1.0 / np.sqrt(D)
        return {'entity_emb': jax.random.normal(ks[0], (N, D), jnp.float32) * s, 'basis1': jax.random.normal(ks[1], (B, D, D), jnp.float32) * s, 'comp1': jax.random.normal(ks[2], (R, B), jnp.float32) * 0.3, 'loop_w1': jax.random.normal(ks[3], (D, D), jnp.float32) * s, 'bias1': jnp.zeros((D,), jnp.float32), 'basis2': jax.random.normal(ks[4], (B, D, D), jnp.float32) * s, 'comp2': jax.random.normal(ks[5], (R, B), jnp.float32) * 0.3, 'loop_w2': jax.random.normal(ks[6], (D, D), jnp.float32) * s, 'bias2': jnp.zeros((D,), jnp.float32), 'ln_g': jnp.ones((D,), jnp.float32), 'ln_b': jnp.zeros((D,), jnp.float32), 'etimes': jax.random.uniform(ks[7], (E,), jnp.float32), 'current_time': jnp.float32(1.0), 'src': jax.random.randint(ks[8], (E,), 0, N), 'dst': jax.random.randint(ks[9], (E,), 0, N), 'etypes': jax.random.randint(ks[10], (E,), 0, R)}
    _L0_gnn_all = _L0_gnn_setup()
    _L0_gnn_in = {k: v for k, v in _L0_gnn_all.items() if k in ('basis1', 'comp1', 'loop_w1', 'bias1', 'basis2', 'comp2', 'loop_w2', 'bias2', 'ln_g', 'ln_b', 'current_time')}
    del _L0_gnn_all
    return {'x': x, 'src': src, 'dst': dst, 'edge_type_240': edge_type_240, 'edge_weight': edge_weight, 'L0_gnn_basis1': _L0_gnn_in['basis1'], 'L0_gnn_comp1': _L0_gnn_in['comp1'], 'L0_gnn_loop_w1': _L0_gnn_in['loop_w1'], 'L0_gnn_bias1': _L0_gnn_in['bias1'], 'L0_gnn_basis2': _L0_gnn_in['basis2'], 'L0_gnn_comp2': _L0_gnn_in['comp2'], 'L0_gnn_loop_w2': _L0_gnn_in['loop_w2'], 'L0_gnn_bias2': _L0_gnn_in['bias2'], 'L0_gnn_ln_g': _L0_gnn_in['ln_g'], 'L0_gnn_ln_b': _L0_gnn_in['ln_b'], 'L0_gnn_current_time': _L0_gnn_in['current_time']}

def reference(x, src, dst, edge_type_240, edge_weight, L0_gnn_basis1, L0_gnn_comp1, L0_gnn_loop_w1, L0_gnn_bias1, L0_gnn_basis2, L0_gnn_comp2, L0_gnn_loop_w2, L0_gnn_bias2, L0_gnn_ln_g, L0_gnn_ln_b, L0_gnn_current_time):
    import jax
    import jax.numpy as jnp

    def _L0_gnn_ref(entity_emb, basis1, comp1, loop_w1, bias1, basis2, comp2, loop_w2, bias2, ln_g, ln_b, etimes, current_time, src, dst, etypes):
        import jax, jax.numpy as jnp
        import numpy as np
        N = 50000
        R = 240
        D = 256
        B = 10
        E = 5000
        RATE = 0.1
        LN_EPS = 1e-05

        def _time_decay(etimes, current_time):
            td = jnp.maximum(current_time - etimes, 0.0)
            td = td / (td.max() + 1e-08)
            return jnp.exp(-RATE * td)[:, None]

        def _rgcn_layer(h, basis, comp, loop_w, bias, src, dst, etypes, enorm):
            hsrc = h[src]
            coef = comp[etypes]
            msg = jnp.zeros_like(hsrc)
            for b in range(basis.shape[0]):
                msg = msg + coef[:, b:b + 1] * (hsrc @ basis[b])
            msg = msg * enorm
            agg = jax.ops.segment_sum(msg, dst, num_segments=h.shape[0])
            return agg + bias + h @ loop_w
        enorm = _time_decay(etimes, current_time)
        h_init = entity_emb
        h = h_init
        h = jax.nn.relu(_rgcn_layer(h, basis1, comp1, loop_w1, bias1, src, dst, etypes, enorm))
        h = jax.nn.relu(_rgcn_layer(h, basis2, comp2, loop_w2, bias2, src, dst, etypes, enorm))
        h = h + h_init
        mu = h.mean(-1, keepdims=True)
        var = ((h - mu) ** 2).mean(-1, keepdims=True)
        return (h - mu) * jax.lax.rsqrt(var + LN_EPS) * ln_g + ln_b
    h = jnp.maximum(_layernorm(x, axis=-1), 0.0)
    x = x + _L0_gnn_ref(h, L0_gnn_basis1, L0_gnn_comp1, L0_gnn_loop_w1, L0_gnn_bias1, L0_gnn_basis2, L0_gnn_comp2, L0_gnn_loop_w2, L0_gnn_bias2, L0_gnn_ln_g, L0_gnn_ln_b, edge_weight, L0_gnn_current_time, src, dst, edge_type_240)
    return x

_drawn_inputs = setup_inputs


def setup_inputs(seed=0):
    import zlib

    import numpy as np

    out = dict(_drawn_inputs(seed))
    spreads = {'L0_gnn_bias1': (0.0, 0.1),
     'L0_gnn_bias2': (0.0, 0.1),
     'L0_gnn_ln_g': (1.0, 0.2),
     'L0_gnn_ln_b': (0.0, 0.1)}
    factors = {}
    for name, (base, spread) in spreads.items():
        noise = np.random.default_rng([zlib.crc32(name.encode()), seed]).standard_normal(out[name].shape)
        drawn = base * np.exp(spread * noise) if base else spread * noise
        out[name] = jnp.asarray(drawn.astype(out[name].dtype))
    for name, factor in factors.items():
        out[name] = (out[name] * factor).astype(out[name].dtype)
    return out
```

```python
from contextlib import ExitStack

import concourse.bass as bass
from concourse import mybir

ALU = mybir.AluOpType
ACT = mybir.ActivationFunctionType
AX = mybir.AxisListType
F32 = mybir.dt.float32
F32R = mybir.dt.float32r
I32 = mybir.dt.int32
RMAX = bass.bass_isa.ReduceOp.max

P = 128
LN_EPS = 1e-5
RATE = 0.1


def rgcn_kernel(nc, x, src, dst, edge_type, edge_time, basis1, comp1, loop_w1, bias1,
                basis2, comp2, loop_w2, bias2, ln_g, ln_b, current_time, out):
    N, D = x.shape
    E = src.shape[0]
    R, B = comp1.shape
    KH = D // P
    ET = -(-E // P)
    FULL = E // ET
    REST = E - FULL * ET
    TG = 4
    GR = TG * P
    NG = -(-N // GR)
    NQ = NG * TG // 2
    W2 = 2 * D
    NBK = B * D // W2
    CH = 2 * NBK
    assert KH == 2 and W2 == 512 and B == 2 * NBK and NG % 2 == 0 and ET % 2 == 0
    assert FULL == P - 1 and E - FULL * ET > 0

    pre1 = nc.dram_tensor("pre1", (N + P, D), F32, kind="Internal").ap()
    agg2 = nc.dram_tensor("agg2", (N + P, D), F32, kind="Internal").ap()

    def base(g):
        return N - GR if isinstance(g, int) and g == NG - 1 else g * GR

    def rows(t, g):
        return t[bass.ds(base(g), GR), :].rearrange("(p j) d -> p (j d)", p=P)

    with ExitStack() as ctx:
        def sb(name, shape, dt=F32):
            return ctx.enter_context(nc.sbuf_tensor(name, shape, dt))

        def sem(name):
            return ctx.enter_context(nc.semaphore(name))

        ident = sb("ident", [P, P])
        tril = sb("tril", [P, P])
        ones_rows = sb("ones_rows", [P, P], F32R)
        bias_rows = sb("bias_rows", [P, W2], F32R)
        bias_raw = sb("bias_raw", [2, D])
        bias_hi = sb("bias_hi", [2, D])
        bias_hr = sb("bias_hr", [2, D], F32R)
        bias_lo = sb("bias_lo", [2, D])
        agg_init = sb("agg_init", [P, TG, D])
        zero_row = sb("zero_row", [P, D])
        g_bc = sb("g_bc", [P, 2, D])
        b_bc = sb("b_bc", [P, 2, D])
        eps = sb("eps", [P, 1])
        basis_raw = sb("basis_raw", [P, KH, B * D])
        basis_hi = sb("basis_hi", [P, KH, B * D], F32R)
        basis_lo = sb("basis_lo", [P, KH, B * D], F32R)
        loop_raw = sb("loop_raw", [P, 2, KH, D])
        loop_hi = sb("loop_hi", [P, 2, KH, D], F32R)
        loop_lo = sb("loop_lo", [P, 2, KH, D], F32R)
        src_i = sb("src_i", [P, ET], I32)
        type_i = sb("type_i", [P, ET], I32)
        dst_i = sb("dst_i", [P, ET], I32)
        src_type = sb("src_type", [P, ET, 2], I32)
        dst_f = sb("dst_f", [P, ET])
        spare = sb("spare", [P, ET])
        dst_row = sb("dst_row", [P, P, ET], I32)
        etime = sb("etime", [P, ET])
        ctime = sb("ctime", [P, 1])
        decay = sb("decay", [P, ET])
        tmax = sb("tmax", [P, 4])
        rstd = sb("rstd", [P, NG * TG])
        nmr = sb("nmr", [P, NG * TG])
        xg = sb("xg", [P, 2, TG * D])
        zg = sb("zg", [P, 2, TG * D])
        og = sb("og", [P, 2, TG * D])
        ag = sb("ag", [P, 2, TG * D])
        hi = sb("hi", [P, 2, W2], F32R)
        lo = sb("lo", [P, 2, W2], F32R)
        st = sb("st", [P, 4, 6])
        mv = sb("mv", [P, 2, TG, 2])
        std = sb("std", [P, 2, TG])
        xe = sb("xe", [P, 2, D])
        ids = sb("ids", [P, 2, 2], I32)
        cr = sb("cr", [P, 2, B])
        cw = sb("cw", [P, 2, B])
        acc = sb("acc", [P, 2, D])
        msg = sb("msg", [P, 2, D])
        same = sb("same", [P, 2, P])
        junk = sb("junk", [P, P])
        dup = sb("dup", [P, 2])
        magg = sb("magg", [P, 2, D])
        sidx = sb("sidx", [P, 2, 1], I32)
        est = sb("est", [P, 6])
        emv = sb("emv", [P, 2])
        estd = sb("estd", [P, 1])
        enr = sb("enr", [P, 2])
        spot = dst_row[:, :, :].rearrange("q p t -> q (p t)").bitcast(F32)

        def carve(at, n):
            return spot[:, at * W2:(at + n) * W2].rearrange("p (s w) -> p s w", w=W2)

        h0, v, y, yg, xb = carve(0, 2), carve(2, 2), carve(4, 2), carve(6, 2), carve(8, 4)
        u = sb("u", [P, W2])
        cst = sb("cst", [P, 2, 6])
        cmv = sb("cmv", [P, 2, 2])
        cstd = sb("cstd", [P, 2])
        cnr = sb("cnr", [P, 2, 2, 2])

        psT = [ctx.enter_context(nc.psum_tensor(f"psT{i}", [P, W2], F32)) for i in range(2)]
        psM = [ctx.enter_context(nc.psum_tensor(f"psM{i}", [P, W2], F32)) for i in range(NBK)]
        psS = ctx.enter_context(nc.psum_tensor("psS", [P, W2], F32))

        s_w = sem("s_w")
        s_pool_go = sem("s_pool_go")
        s_dve_go = sem("s_dve_go")
        s_small = sem("s_small")
        s_edges = sem("s_edges")
        s_clear = sem("s_clear")
        s_const = sem("s_const")
        s_pool = sem("s_pool")
        s_loop_hi = sem("s_loop_hi")
        s_loop_lo = sem("s_loop_lo")
        s_bias = sem("s_bias")
        s_bias_hi = sem("s_bias_hi")
        s_basis_raw = sem("s_basis_raw")
        s_basis_hi = [sem(f"s_basis_hi{l}") for l in range(2)]
        s_basis_lo = [sem(f"s_basis_lo{l}") for l in range(2)]
        s_td = sem("s_td")
        s_tmax = sem("s_tmax")
        s_exp = sem("s_exp")
        s_dst = sem("s_dst")
        s_dummy = sem("s_dummy")
        s_agg_init = sem("s_agg_init")
        s_agg = sem("s_agg")
        a_x = [sem(f"a_x{i}") for i in range(2)]
        a_st = sem("a_st")
        a_mv = sem("a_mv")
        a_std = sem("a_std")
        a_rstd = sem("a_rstd")
        a_nmr = sem("a_nmr")
        a_z = sem("a_z")
        a_tr = sem("a_tr")
        a_hi = sem("a_hi")
        a_lo = sem("a_lo")
        a_mm = sem("a_mm")
        a_ev = sem("a_ev")
        a_out = [sem(f"a_out{i}") for i in range(2)]
        names = ["ids", "stat", "mv", "std", "rstd", "nmr", "z", "tr", "hi", "lo", "mm", "cw", "comb",
                 "msg", "same", "dup", "dupc", "sidx", "smm", "magg", "scat"]
        e = [{n: sem(f"e{l}_{n}") for n in names} for l in range(2)]
        for l in range(2):
            e[l]["row"] = [sem(f"e{l}_row{i}") for i in range(2)]
            e[l]["coef"] = [sem(f"e{l}_coef{i}") for i in range(2)]
        c_p = [sem(f"c_p{i}") for i in range(2)]
        c_x = [sem(f"c_x{i}") for i in range(2)]
        c_a = [sem(f"c_a{i}") for i in range(2)]
        c_out = [sem(f"c_out{i}") for i in range(2)]
        c_tr = sem("c_tr")
        c_hi = sem("c_hi")
        c_lo = sem("c_lo")
        c_mm = sem("c_mm")
        c_h0 = sem("c_h0")
        c_u = sem("c_u")
        c_v = sem("c_v")
        c_st = sem("c_st")
        c_mv = sem("c_mv")
        c_std = sem("c_std")
        c_rstd = sem("c_rstd")
        c_nmr = sem("c_nmr")
        c_y = sem("c_y")
        c_yg = sem("c_yg")
        c_xb = sem("c_xb")
        c_o = sem("c_o")

        def after(eng, s, count):
            if not isinstance(count, int) or count > 0:
                eng.wait_ge(s, count)

        def ran(i, n):
            return not isinstance(i, int) or 0 <= i < n

        def looped(eng, trips, body, first=1):
            for i in range(first):
                body(i)
            with eng.Fori(first, trips - 1) as it:
                body(it)
            body(trips - 1)

        block = ctx.enter_context(nc.Block())

        def flat(v):
            return v.rearrange("(a n) -> a n", a=1)

        @block.sync
        def _(sp):
            sp.dma_start(loop_raw[:, 0], loop_w1.rearrange("(k p) n -> p k n", p=P)).then_inc(s_w, 16)
            sp.dma_start(loop_raw[:, 1], loop_w2.rearrange("(k p) n -> p k n", p=P)).then_inc(s_w, 16)
            for r in range(2):
                sp.dma_start(bias_raw[r:r + 1, :], flat(bias1)).then_inc(s_small, 16)
            sp.dma_start(ctime[:, :], flat(current_time).to_broadcast([P, 1])).then_inc(s_small, 16)
            for j in range(2):
                sp.dma_start(g_bc[:, j, :], flat(ln_g).to_broadcast([P, D])).then_inc(s_small, 16)
                sp.dma_start(b_bc[:, j, :], flat(ln_b).to_broadcast([P, D])).then_inc(s_small, 16)

            def load_x(it):
                for s in range(2):
                    g = 2 * it + s
                    after(sp, a_z, g - 1)
                    sp.dma_start(xg[:, s], rows(x, g)).then_inc(a_x[s], 16)
                    if isinstance(it, int) and it == 0 and s == 1:
                        for j in range(TG):
                            sp.dma_start(agg_init[:, j, :], flat(bias2).to_broadcast([P, D])).then_inc(s_agg_init, 16)
                        sp.wait_ge(s_clear, 5)
                        for t, v in ((src_i, src), (type_i, edge_type), (dst_i, dst), (etime, edge_time)):
                            sp.dma_start(t[0:FULL, :], v[0:FULL * ET].rearrange("(p t) -> p t", t=ET)).then_inc(s_edges, 16)
                            sp.dma_start(t[FULL:P, 0:REST], flat(v[FULL * ET:E])).then_inc(s_edges, 16)
                        sp.dma_start(dst_row[:, :, :].rearrange("q p t -> q (p t)")[:, 0:E],
                                     flat(dst).to_broadcast([P, E])).then_inc(s_edges, 16)
                        sp.dma_start(basis_raw[:, 0], basis1[:, 0:P, :].rearrange("b p n -> p b n")).then_inc(s_basis_raw, 16)
                        sp.dma_start(basis_raw[:, 1], basis1[:, P:D, :].rearrange("b p n -> p b n")).then_inc(s_basis_raw, 16)

            looped(sp, NG // 2, load_x)

            sp.wait_ge(s_agg_init, 16 * TG)

            def init_agg(it):
                for s in range(2):
                    g = 2 * it + s
                    if isinstance(g, int) and g == NG - 1:
                        sp.wait_ge(s_agg, 16 * (NG - 1))
                    sp.dma_start(rows(agg2, g), agg_init[:, :, :].rearrange("p j d -> p (j d)")).then_inc(s_agg, 16)

            looped(sp, NG // 2, init_agg)

            sp.wait_ge(s_basis_hi[0], KH)
            sp.wait_ge(s_basis_lo[0], KH)
            sp.dma_start(basis_raw[:, 0], basis2[:, 0:P, :].rearrange("b p n -> p b n")).then_inc(s_basis_raw, 16)
            sp.dma_start(basis_raw[:, 1], basis2[:, P:D, :].rearrange("b p n -> p b n")).then_inc(s_basis_raw, 16)

            def load_c(it):
                for s in range(2):
                    g = 2 * it + s
                    after(sp, c_tr, 2 * g - 2)
                    sp.dma_start(zg[:, s], rows(pre1, g)).then_inc(c_p[s], 16)
                    after(sp, c_xb, 2 * g - 2)
                    after(sp, c_h0, 2 * g - 2)
                    sp.dma_start(xg[:, s], rows(x, g)).then_inc(c_x[s], 16)
                    after(sp, c_u, 2 * g - 2)
                    sp.dma_start(ag[:, s], rows(agg2, g)).then_inc(c_a[s], 16)

            sp.wait_ge(e[0]["scat"], 16 * ET)
            sp.wait_ge(e[1]["z"], 1)
            sp.wait_ge(e[1]["scat"], 16 * ET)
            looped(sp, NG // 2, load_c)
            sp.wait_ge(c_out[0], 16 * (NG // 2))
            sp.wait_ge(c_out[1], 16 * (NG // 2))

        @block.gpsimd
        def _(pool):
            pool.memset(ident[:], 0.0).then_inc(s_pool, 1)
            pool.memset(tril[:], 1.0).then_inc(s_pool, 1)
            pool.memset(ones_rows[:].bitcast(F32), 0.0).then_inc(s_pool, 1)
            pool.wait_ge(s_pool, 3)
            pool.affine_select(out=ident[:], in_=ident[:], compare_op=ALU.not_equal, fill=1.0, base=0,
                               pattern=[[-1, P]], channel_multiplier=1).then_inc(s_const, 1)
            pool.affine_select(out=tril[:], in_=tril[:], compare_op=ALU.is_gt, fill=0.0, base=0,
                               pattern=[[-1, P]], channel_multiplier=1).then_inc(s_const, 1)
            pool.memset(ones_rows[0:2, :].bitcast(F32), 1.0).then_inc(s_const, 1)
            pool.memset(eps[:], LN_EPS).then_inc(s_const, 1)
            pool.memset(bias_rows[:].bitcast(F32), 0.0).then_inc(s_const, 1)
            pool.memset(src_i[:], 0).then_inc(s_clear, 1)
            pool.memset(type_i[:], 0).then_inc(s_clear, 1)
            pool.memset(dst_i[:], N + P - 1).then_inc(s_clear, 1)
            pool.memset(etime[:], 3.0e38).then_inc(s_clear, 1)
            pool.memset(dst_row[:, FULL, :], N + P - 1).then_inc(s_clear, 1)
            pool.memset(zero_row[:], 0.0).then_inc(s_dst, 1)
            pool.iota(spare[:], pattern=[[0, ET]], base=N, channel_multiplier=1,
                      allow_small_or_imprecise_dtypes=True).then_inc(s_dst, 1)
            pool.wait_ge(s_dst, 1)
            for t in (pre1, agg2):
                pool.dma_start(t[N:N + P, :], zero_row[:]).then_inc(s_dummy, 16)
            pool.wait_ge(s_edges, 16 * 9)
            pool.tensor_copy(src_type[:, :, 0], src_i[:]).then_inc(s_pool, 1)
            pool.tensor_copy(src_type[:, :, 1], type_i[:]).then_inc(s_pool, 1)
            pool.wait_ge(s_pool, 5)
            pool.wait_ge(s_td, 3)
            pool.partition_all_reduce(tmax[:, 1:2], tmax[:, 0:1], P, RMAX).then_inc(s_tmax, 1)

            for l in range(2):
                el = e[l]
                table = x if l == 0 else pre1
                comp = comp1 if l == 0 else comp2
                target = pre1 if l == 0 else agg2
                if l == 0:
                    pool.wait_ge(s_dummy, 32)
                else:
                    pool.wait_ge(e[0]["scat"], 16 * ET)
                    pool.wait_ge(e[0]["cw"], ET)
                    pool.wait_ge(e[0]["tr"], ET)

                def gather(t, s):
                    after(pool, el["row"][s], 16 * (t // 2) if isinstance(t, int) else 16 * half)
                    after(pool, el["coef"][s], 16 * (t // 2) if isinstance(t, int) else 16 * half)
                    pool.tensor_copy(ids[:, s], src_type[:, bass.ds(t, 1), :].rearrange("p a b -> p (a b)")).then_inc(el["ids"], 1)
                    pool.wait_ge(el["ids"], t + 1)
                    after(pool, el["tr"], t - 1)
                    pool.sem_inc(s_pool_go, 1)
                    pool.indirect_dma_start(out=xe[:, s], out_offset=None, in_=table[:, :],
                                            in_offset=bass.IndirectOffsetOnAxis(ap=ids[:, s, 0:1], axis=0)
                                            ).then_inc(el["row"][s], 16)
                    after(pool, el["cw"], t - 1)
                    pool.sem_inc(s_pool_go, 1)
                    pool.indirect_dma_start(out=cr[:, s], out_offset=None, in_=comp[:, :],
                                            in_offset=bass.IndirectOffsetOnAxis(ap=ids[:, s, 1:2], axis=0)
                                            ).then_inc(el["coef"][s], 16)

                def scatter(t, s):
                    after(pool, el["scat"], 16 * t)
                    if l == 0 and isinstance(t, int) and t == 0:
                        pool.wait_ge(a_out[0], 16 * (NG // 2))
                        pool.wait_ge(a_out[1], 16 * (NG // 2))
                    if l == 1 and isinstance(t, int) and t == 0:
                        pool.wait_ge(s_agg, 16 * NG)
                    pool.wait_ge(el["magg"], t + 1)
                    pool.wait_ge(el["sidx"], t + 1)
                    pool.sem_inc(s_pool_go, 1)
                    pool.indirect_dma_start(out=target[:, :],
                                            out_offset=bass.IndirectOffsetOnAxis(ap=sidx[:, s, :], axis=0),
                                            in_=magg[:, s], in_offset=None, compute_op=ALU.add
                                            ).then_inc(el["scat"], 16)

                half = 0
                gather(0, 0)
                gather(1, 1)

                def edges(it):
                    nonlocal half
                    for s in range(2):
                        t = 2 * it + s
                        half = it + 1
                        if not (isinstance(t, int) and t + 2 >= ET):
                            gather(t + 2, s)
                        if ran(t - 1, ET):
                            scatter(t - 1, 1 - s)

                looped(pool, ET // 2, edges)
                scatter(ET - 1, (ET - 1) % 2)

            def nodes_c(it):
                for k in range(4):
                    q = 4 * it + k
                    if ran(q, NQ):
                        s = (k // 2) % 2
                        if k % 2 == 0:
                            pool.wait_ge(c_x[s], 16 * (it + 1))
                        after(pool, c_o, q - 3)
                        pool.tensor_tensor(xb[:, k], xg[:, s, (k % 2) * W2:(k % 2 + 1) * W2],
                                           b_bc[:, :, :].rearrange("p j d -> p (j d)"), ALU.add).then_inc(c_xb, 1)
                    if ran(q - 2, NQ):
                        pool.wait_ge(c_y, q - 1)
                        after(pool, c_o, q - 3)
                        pool.tensor_tensor(yg[:, k % 2], y[:, k % 2],
                                           g_bc[:, :, :].rearrange("p j d -> p (j d)"), ALU.mult).then_inc(c_yg, 1)

            looped(pool, NQ // 4, nodes_c)
            nodes_c(NQ // 4)

        @block.tensor
        def _(pe):
            pe.wait_ge(s_const, 5)
            pe.wait_ge(s_bias, 2)
            pe.wait_ge(s_loop_hi, 1)
            pe.wait_ge(s_loop_lo, 1)

            def transposes(bank, tile, done):
                n = tile.shape[1] // P
                for i in range(n):
                    last = pe.transpose(psT[bank][:, i * P:(i + 1) * P], tile[:, i * P:(i + 1) * P], ident[:])
                last.then_inc(done, 1)

            def node_products(layer, b, biased, done):
                if biased:
                    pe.matmul(psM[b][:], ones_rows[:], bias_rows[:], start=True, stop=False, skip_group_check=True)
                for j in range(2):
                    o = psM[b][:, j * D:(j + 1) * D]
                    n = 0
                    for kh in range(KH):
                        c = (j * KH + kh) * P
                        for h, w in ((hi, loop_hi), (hi, loop_lo), (lo, loop_hi)):
                            last = pe.matmul(o, h[:, b, c:c + P], w[:, layer, kh, :],
                                             start=(n == 0 and not biased), stop=(n == 3 * KH - 1), skip_group_check=True)
                            n += 1
                last.then_inc(done, 1)

            def nodes(it, phase):
                tr, hi_s, lo_s, mm_s, done_prev = ((a_tr, a_hi, a_lo, a_mm, a_ev) if phase == "A"
                                                   else (c_tr, c_hi, c_lo, c_mm, c_u))
                for k in range(4):
                    q = 4 * it + k
                    if ran(q, NQ):
                        s = k // 2
                        if k % 2 == 0:
                            if phase == "A":
                                pe.wait_ge(a_z, 2 * it + s + 1)
                            else:
                                pe.wait_ge(c_p[s], 16 * (it + 1))
                        after(pe, hi_s, q - 1)
                        after(pe, lo_s, q - 1)
                        transposes(k % 2, zg[:, s, (k % 2) * W2:(k % 2 + 1) * W2], tr)
                    if ran(q - 1, NQ):
                        pe.wait_ge(hi_s, q)
                        pe.wait_ge(lo_s, q)
                        after(pe, done_prev, q - 2)
                        node_products(0 if phase == "A" else 1, (k - 1) % 2, phase == "A", mm_s)

            def nodes_a(it):
                nodes(it, "A")

            def nodes_c(it):
                nodes(it, "C")

            looped(pe, NQ // 4, nodes_a)
            nodes_a(NQ // 4)

            for l in range(2):
                el = e[l]

                def transpose_edges(t, s, half):
                    if l == 0:
                        pe.wait_ge(el["z"], t + 1)
                    else:
                        pe.wait_ge(el["row"][s], 16 * half)
                    transposes(s, xe[:, s], el["tr"])

                def combine_duplicates(t, s):
                    pe.wait_ge(el["same"], t + 1)
                    pe.wait_ge(el["msg"], t + 1)
                    after(pe, el["magg"], t)
                    pe.matmul(psS[:, 0:D], same[:, s], msg[:, s], start=True, stop=True).then_inc(el["smm"], 1)

                if l == 0:
                    pe.wait_ge(a_ev, NQ)
                else:
                    pe.wait_ge(e[0]["magg"], ET)
                transpose_edges(0, 0, 1)
                pe.wait_ge(s_basis_hi[l], KH)
                pe.wait_ge(s_basis_lo[l], KH)

                def edges(it):
                    for s in range(2):
                        t = 2 * it + s
                        for b in range(NBK):
                            if b == 0:
                                pe.wait_ge(el["hi"], t + 1)
                                pe.wait_ge(el["lo"], t + 1)
                            after(pe, el["comb"], CH * (t - 1) + 2 * b + 2)
                            n = 0
                            for kh in range(KH):
                                for h, w in ((hi, basis_hi), (hi, basis_lo), (lo, basis_hi)):
                                    last = pe.matmul(psM[b][:], h[:, s, kh * P:(kh + 1) * P],
                                                     w[:, kh, b * W2:(b + 1) * W2], start=(n == 0), stop=(n == 3 * KH - 1))
                                    n += 1
                            last.then_inc(el["mm"], 1)
                            if b == 0 and not (isinstance(t, int) and t + 1 >= ET):
                                transpose_edges(t + 1, 1 - s, it + 1 if s == 0 else it + 2)
                            if b == 1 and ran(t - 1, ET):
                                combine_duplicates(t - 1, 1 - s)

                looped(pe, ET // 2, edges)
                combine_duplicates(ET - 1, (ET - 1) % 2)

            pe.wait_ge(e[1]["magg"], ET)
            looped(pe, NQ // 4, nodes_c)
            nodes_c(NQ // 4)

        @block.scalar
        def _(act):
            act.wait_ge(s_w, 32)
            act.activation(loop_hi[:], loop_raw[:], ACT.Copy).then_inc(s_loop_hi, 1)
            act.wait_ge(s_small, 16 * 7)
            act.activation(bias_hr[:], bias_raw[:], ACT.Copy).then_inc(s_bias_hi, 1)
            act.wait_ge(s_const, 5)

            def split_hi(s, w, done):
                act.activation(hi[:, s, 0:w], psT[s][:, 0:w], ACT.Relu).then_inc(done, 1)

            def std_a(g, s):
                act.wait_ge(a_mv, g + 1)
                act.activation(std[:, s], mv[:, s, :, 1], ACT.Sqrt, bias=eps[:]).then_inc(a_std, 1)

            def nodes_a(it):
                for s in range(2):
                    g = 2 * it + s
                    for k in range(2):
                        q = 2 * g + k
                        if ran(g, NG):
                            act.wait_ge(a_tr, q + 1)
                            after(act, a_mm, q - 1)
                            split_hi(k, W2, a_hi)
                        if ran(q - 1, NQ):
                            ps = s if k == 1 else 1 - s
                            if k == 1:
                                after(act, a_out[ps], 16 * it)
                            act.wait_ge(a_mm, q)
                            act.activation(og[:, ps, (1 - k) * W2:(2 - k) * W2], psM[1 - k][:], ACT.Copy).then_inc(a_ev, 1)
                            if k == 0:
                                act.wait_ge(a_ev, q)
                                act.dma_start(rows(pre1, g - 1), og[:, ps]).then_inc(a_out[ps], 16)
                        if k == 0 and not (isinstance(g, int) and g + 1 >= NG):
                            std_a(g + 1, 1 - s)

            std_a(0, 0)
            looped(act, NG // 2, nodes_a)
            act.wait_ge(a_mm, NQ)
            act.activation(og[:, 1, W2:2 * W2], psM[1][:], ACT.Copy).then_inc(a_ev, 1)
            act.wait_ge(a_ev, NQ)
            act.wait_ge(a_out[0], 16 * (NG // 2))
            act.dma_start(rows(pre1, NG - 1), og[:, 1]).then_inc(a_out[1], 16)
            act.wait_ge(s_td, 8)
            act.activation(decay[:], etime[:], ACT.Exp, scale=-RATE).then_inc(s_exp, 1)

            for l in range(2):
                el = e[l]

                def std_e(t):
                    act.wait_ge(el["mv"], t + 1)
                    act.activation(estd[:], emv[:, 1:2], ACT.Sqrt, bias=eps[:]).then_inc(el["std"], 1)

                def hi_e(t, s):
                    act.wait_ge(el["tr"], t + 1)
                    after(act, el["mm"], NBK * (t - 1))
                    split_hi(s, D, el["hi"])

                def magg_e(t, s):
                    act.wait_ge(el["smm"], t + 1)
                    after(act, el["scat"], 16 * (t - 1))
                    act.activation(magg[:, s], psS[:, 0:D], ACT.Copy).then_inc(el["magg"], 1)

                if l == 0:
                    act.wait_ge(s_basis_raw, 32)
                else:
                    act.wait_ge(s_basis_raw, 64)
                    act.wait_ge(e[0]["mm"], NBK * ET)
                for kh in range(KH):
                    act.activation(basis_hi[:, kh], basis_raw[:, kh], ACT.Copy).then_inc(s_basis_hi[l], 1)
                if l == 0:
                    std_e(0)
                hi_e(0, 0)
                if l == 0:
                    std_e(1)

                def edges(it):
                    for s in range(2):
                        t = 2 * it + s
                        if not (isinstance(t, int) and t + 1 >= ET):
                            hi_e(t + 1, 1 - s)
                        if ran(t - 1, ET):
                            magg_e(t - 1, 1 - s)
                        if l == 0 and not (isinstance(t, int) and t + 2 >= ET):
                            std_e(t + 2)

                looped(act, ET // 2, edges)
                magg_e(ET - 1, (ET - 1) % 2)

            def nodes_c(it):
                for k in range(4):
                    q = 4 * it + k
                    if ran(q, NQ):
                        act.wait_ge(c_tr, q + 1)
                        after(act, c_mm, q - 1)
                        split_hi(k % 2, W2, c_hi)
                        if k % 2 == 0:
                            act.wait_ge(c_x[k // 2], 16 * (it + 1))
                        after(act, c_v, q - 1)
                        for j in range(2):
                            c = 8 * it + 2 * k + j
                            a = (k % 2) * W2 + j * D
                            last = act.activation(h0[:, k % 2, j * D:(j + 1) * D], xg[:, k // 2, a:a + D], ACT.Relu,
                                                  bias=nmr[:, bass.ds(c, 1)], scale=rstd[:, bass.ds(c, 1)])
                        last.then_inc(c_h0, 1)
                    if ran(q - 2, NQ):
                        act.wait_ge(c_nmr, q - 1)
                        after(act, c_yg, q - 3)
                        for j in range(2):
                            last = act.activation(y[:, k % 2, j * D:(j + 1) * D], v[:, k % 2, j * D:(j + 1) * D], ACT.Identity,
                                                  bias=cnr[:, k % 2, 1, j:j + 1], scale=cnr[:, k % 2, 0, j:j + 1])
                        last.then_inc(c_y, 1)
                    if ran(q - 1, NQ):
                        act.wait_ge(c_mv, q)
                        act.activation(cstd[:], cmv[:, :, 1], ACT.Sqrt, bias=eps[:]).then_inc(c_std, 1)
                    if k % 2 == 1:
                        g, s = 2 * it - 2 + k // 2, k // 2
                        if ran(g, NG):
                            act.wait_ge(c_o, 2 * g + 2)
                            if isinstance(g, int) and g == NG - 1:
                                act.wait_ge(c_out[0], 16 * (NG // 2))
                            act.dma_start(rows(out, g), og[:, s]).then_inc(c_out[s], 16)

            looped(act, NQ // 4, nodes_c)
            nodes_c(NQ // 4)

        @block.vector
        def _(dve):
            dve.wait_ge(s_loop_hi, 1)
            dve.tensor_tensor(loop_lo[:], loop_raw[:], loop_hi[:].bitcast(F32), ALU.subtract).then_inc(s_loop_lo, 1)
            dve.wait_ge(s_bias_hi, 1)
            dve.wait_ge(s_const, 5)
            dve.tensor_tensor(bias_lo[:], bias_raw[:], bias_hr[:].bitcast(F32), ALU.subtract).then_inc(s_bias_hi, 1)
            dve.wait_ge(s_bias_hi, 2)
            dve.tensor_scalar(bias_hi[:], bias_lo[:], ident[0:2, 1:2], None, ALU.mult).then_inc(s_bias_hi, 1)
            dve.wait_ge(s_bias_hi, 3)
            for j in range(2):
                dve.scalar_tensor_tensor(out=bias_rows[0:2, j * D:(j + 1) * D], in0=bias_hr[:].bitcast(F32),
                                         scalar=ident[0:2, 0:1], in1=bias_hi[:], op0=ALU.mult, op1=ALU.add).then_inc(s_bias, 1)

            def split_lo(s, w, done):
                dve.scalar_tensor_tensor(out=lo[:, s, 0:w], in0=psT[s][:, 0:w], scalar=0.0, in1=hi[:, s, 0:w].bitcast(F32),
                                         op0=ALU.max, op1=ALU.subtract).then_inc(done, 1)

            def stats_a(g, s, half):
                dve.wait_ge(a_x[s], 16 * half)
                after(dve, a_mv, g)
                for j in range(TG):
                    last = dve.bn_stats(st[:, j], xg[:, s, j * D:(j + 1) * D])
                last.then_inc(a_st, 1)
                dve.wait_ge(a_st, g + 1)
                after(dve, a_nmr, g - 1)
                dve.sem_inc(s_dve_go, 1)
                for j in range(TG):
                    last = dve.bn_aggr(mv[:, s, j], st[:, j])
                last.then_inc(a_mv, 1)

            def norm_a(g, s):
                dve.wait_ge(a_std, g + 1)
                c = bass.ds(g * TG, TG)
                dve.reciprocal(rstd[:, c], std[:, s]).then_inc(a_rstd, 1)
                dve.wait_ge(a_rstd, g + 1)
                dve.scalar_tensor_tensor(out=nmr[:, c], in0=mv[:, s, :, 0], scalar=-1.0, in1=rstd[:, c],
                                         op0=ALU.mult, op1=ALU.mult).then_inc(a_nmr, 1)
                dve.wait_ge(a_nmr, g + 1)
                after(dve, a_tr, 2 * (g - 1))
                for j in range(TG):
                    o = slice(j * D, (j + 1) * D)
                    last = dve.tensor_scalar(zg[:, s, o], xg[:, s, o], rstd[:, bass.ds(g * TG + j, 1)],
                                             nmr[:, bass.ds(g * TG + j, 1)], ALU.mult, ALU.add)
                last.then_inc(a_z, 1)

            stats_a(0, 0, 1)
            norm_a(0, 0)

            def nodes_a(it):
                for s in range(2):
                    g = 2 * it + s
                    nxt = not (isinstance(g, int) and g + 1 >= NG)
                    for k in range(2):
                        q = 2 * g + k
                        dve.wait_ge(a_hi, q + 1)
                        split_lo(k, W2, a_lo)
                        if k == 0 and nxt:
                            stats_a(g + 1, 1 - s, it + 1 if s == 0 else it + 2)
                    if nxt:
                        norm_a(g + 1, 1 - s)

            looped(dve, NG // 2, nodes_a)

            dve.wait_ge(s_edges, 16 * 9)
            dve.wait_ge(s_small, 16 * 7)
            dve.tensor_scalar(decay[:], etime[:], -1.0, ctime[:], ALU.mult, ALU.add).then_inc(s_td, 1)
            dve.wait_ge(s_td, 1)
            dve.tensor_scalar(decay[:], decay[:], 0.0, None, ALU.max).then_inc(s_td, 1)
            dve.wait_ge(s_td, 2)
            dve.tensor_reduce(tmax[:, 0:1], decay[:], AX.X, ALU.max).then_inc(s_td, 1)
            dve.wait_ge(s_tmax, 1)
            dve.tensor_scalar(tmax[:, 2:3], tmax[:, 1:2], 1e-8, None, ALU.add).then_inc(s_td, 1)
            dve.wait_ge(s_td, 4)
            dve.reciprocal(tmax[:, 3:4], tmax[:, 2:3]).then_inc(s_td, 1)
            dve.wait_ge(s_td, 5)
            dve.tensor_scalar(etime[:], decay[:], tmax[:, 3:4], None, ALU.mult).then_inc(s_td, 1)
            dve.wait_ge(s_dst, 2)
            dve.tensor_copy(dst_f[:], dst_i[:]).then_inc(s_td, 1)
            dve.wait_ge(s_td, 7)
            dve.tensor_tensor(spare[:], spare[:], dst_f[:], ALU.subtract).then_inc(s_td, 1)
            dve.wait_ge(s_td, 8)
            dve.wait_ge(s_exp, 1)

            for l in range(2):
                el = e[l]

                def stats_e(t, s, half):
                    dve.wait_ge(el["row"][s], 16 * half)
                    dve.bn_stats(est[:], xe[:, s]).then_inc(el["stat"], 1)
                    dve.wait_ge(el["stat"], t + 1)
                    dve.sem_inc(s_dve_go, 1)
                    dve.bn_aggr(emv[:], est[:]).then_inc(el["mv"], 1)

                def norm_e(t, s):
                    dve.wait_ge(el["std"], t + 1)
                    dve.reciprocal(enr[:, 0:1], estd[:]).then_inc(el["rstd"], 1)
                    dve.wait_ge(el["rstd"], t + 1)
                    dve.scalar_tensor_tensor(out=enr[:, 1:2], in0=emv[:, 0:1], scalar=-1.0, in1=enr[:, 0:1],
                                             op0=ALU.mult, op1=ALU.mult).then_inc(el["nmr"], 1)
                    dve.wait_ge(el["nmr"], t + 1)
                    dve.tensor_scalar(xe[:, s], xe[:, s], enr[:, 0:1], enr[:, 1:2], ALU.mult, ALU.add).then_inc(el["z"], 1)

                def lo_e(t, s):
                    dve.wait_ge(el["hi"], t + 1)
                    split_lo(s, D, el["lo"])

                if l == 1:
                    dve.wait_ge(s_basis_raw, 64)
                for kh in range(KH):
                    dve.wait_ge(s_basis_hi[l], kh + 1)
                    dve.tensor_tensor(basis_lo[:, kh], basis_raw[:, kh], basis_hi[:, kh].bitcast(F32),
                                      ALU.subtract).then_inc(s_basis_lo[l], 1)
                if l == 0:
                    stats_e(0, 0, 1)
                    norm_e(0, 0)
                else:
                    dve.nop().then_inc(el["z"], 1)
                lo_e(0, 0)
                if l == 0:
                    stats_e(1, 1, 1)
                    norm_e(1, 1)

                def edges(it):
                    for s in range(2):
                        t = 2 * it + s
                        dve.wait_ge(el["coef"][s], 16 * (it + 1))
                        dve.tensor_scalar(cw[:, s], cr[:, s], decay[:, bass.ds(t, 1)], None, ALU.mult).then_inc(el["cw"], 1)
                        dve.wait_ge(el["cw"], t + 1)
                        for b in range(NBK):
                            dve.wait_ge(el["mm"], NBK * t + b + 1)
                            for j in range(2):
                                n = 2 * b + j
                                m = psM[b][:, j * D:(j + 1) * D]
                                w = cw[:, s, n:n + 1]
                                if b == 0:
                                    after(dve, el["msg"], t)
                                    dve.tensor_scalar(acc[:, j], m, w, None, ALU.mult).then_inc(el["comb"], 1)
                                else:
                                    dve.wait_ge(el["comb"], CH * t + n - 1)
                                    dve.scalar_tensor_tensor(out=acc[:, j], in0=m, scalar=w, in1=acc[:, j],
                                                             op0=ALU.mult, op1=ALU.add).then_inc(el["comb"], 1)
                            if b == 1 and not (isinstance(t, int) and t + 1 >= ET):
                                lo_e(t + 1, 1 - s)
                            if b == NBK - 2 and l == 0 and not (isinstance(t, int) and t + 2 >= ET):
                                stats_e(t + 2, s, it + 2)
                        dve.wait_ge(el["comb"], CH * (t + 1))
                        after(dve, el["smm"], t - 1)
                        dve.tensor_tensor(msg[:, s], acc[:, 0], acc[:, 1], ALU.add).then_inc(el["msg"], 1)
                        dve.tensor_scalar(same[:, s], dst_row[:, :, bass.ds(t, 1)].rearrange("q p t -> q (p t)"),
                                          dst_f[:, bass.ds(t, 1)], None, ALU.is_equal).then_inc(el["same"], 1)
                        dve.wait_ge(el["same"], t + 1)
                        after(dve, el["dupc"], t)
                        dve.tensor_tensor_reduce(out=junk[:], in0=same[:, s], in1=tril[:], scale=1.0, scalar=0.0,
                                                 op0=ALU.mult, op1=ALU.add, accum_out=dup[:, 0:1]).then_inc(el["dup"], 1)
                        dve.wait_ge(el["dup"], t + 1)
                        after(dve, el["sidx"], t)
                        dve.tensor_scalar(dup[:, 1:2], dup[:, 0:1], 1.0, spare[:, bass.ds(t, 1)], ALU.min, ALU.mult
                                          ).then_inc(el["dupc"], 1)
                        dve.wait_ge(el["dupc"], t + 1)
                        after(dve, el["scat"], 16 * (t - 1))
                        dve.tensor_tensor(sidx[:, s], dup[:, 1:2], dst_f[:, bass.ds(t, 1)], ALU.add).then_inc(el["sidx"], 1)
                        if l == 0 and not (isinstance(t, int) and t + 2 >= ET):
                            norm_e(t + 2, s)

                looped(dve, ET // 2, edges)

            def nodes_c(it):
                for k in range(4):
                    q = 4 * it + k
                    if ran(q, NQ):
                        dve.wait_ge(c_hi, q + 1)
                        split_lo(k % 2, W2, c_lo)
                    if ran(q - 1, NQ):
                        b = (k - 1) % 2
                        s = ((k - 1) // 2) % 2
                        dve.wait_ge(c_mm, q)
                        if b == 0:
                            dve.wait_ge(c_a[s], 16 * (it + 1))
                        after(dve, c_v, q - 1)
                        dve.tensor_tensor(u[:], psM[b][:], ag[:, s, b * W2:(b + 1) * W2], ALU.add).then_inc(c_u, 1)
                        dve.wait_ge(c_u, q)
                        dve.wait_ge(c_h0, q)
                        after(dve, c_y, q - 2)
                        dve.scalar_tensor_tensor(out=v[:, b], in0=u[:], scalar=0.0, in1=h0[:, b],
                                                 op0=ALU.max, op1=ALU.add).then_inc(c_v, 1)
                        dve.wait_ge(c_v, q)
                        after(dve, c_mv, q - 1)
                        for j in range(2):
                            last = dve.bn_stats(cst[:, j], v[:, b, j * D:(j + 1) * D])
                        last.then_inc(c_st, 1)
                        dve.wait_ge(c_st, q)
                        after(dve, c_nmr, q - 1)
                        dve.sem_inc(s_dve_go, 1)
                        for j in range(2):
                            last = dve.bn_aggr(cmv[:, j], cst[:, j])
                        last.then_inc(c_mv, 1)
                    if ran(q - 3, NQ):
                        s = ((k - 3) // 2) % 2
                        dve.wait_ge(c_yg, q - 2)
                        dve.wait_ge(c_xb, q - 2)
                        if (k - 3) % 2 == 0:
                            done = it if k == 3 else it - 1
                            after(dve, c_out[s], 16 * done)
                        o = ((k - 3) % 2) * W2
                        dve.tensor_tensor(og[:, s, o:o + W2], yg[:, (k - 3) % 2], xb[:, (k - 3) % 4], ALU.add).then_inc(c_o, 1)
                    if ran(q - 1, NQ):
                        dve.wait_ge(c_std, q)
                        after(dve, c_y, q - 2)
                        dve.reciprocal(cnr[:, b, 0], cstd[:]).then_inc(c_rstd, 1)
                        dve.wait_ge(c_rstd, q)
                        dve.scalar_tensor_tensor(out=cnr[:, b, 1], in0=cmv[:, :, 0], scalar=-1.0, in1=cnr[:, b, 0],
                                                 op0=ALU.mult, op1=ALU.mult).then_inc(c_nmr, 1)

            looped(dve, NQ // 4, nodes_c, first=2)
            nodes_c(NQ // 4)


_INS = ['x', 'src', 'dst', 'edge_type_240', 'edge_weight', 'L0_gnn_basis1', 'L0_gnn_comp1', 'L0_gnn_loop_w1',
        'L0_gnn_bias1', 'L0_gnn_basis2', 'L0_gnn_comp2', 'L0_gnn_loop_w2', 'L0_gnn_bias2', 'L0_gnn_ln_g',
        'L0_gnn_ln_b', 'L0_gnn_current_time']


def kernel(**inputs):
    import numpy as _np
    import concourse.bacc as _bacc
    from concourse import mybir as _mybir
    from concourse.bass_utils import run_bass_kernel_spmd as _run

    nc = _bacc.Bacc("TRN2", target_bir_lowering=False, num_devices=1)
    arrays, args = {}, []
    for name in _INS:
        a = _np.ascontiguousarray(inputs[name])
        if a.ndim == 0:
            a = a.reshape(1)
        arrays[f"in_{name}_dram"] = a
        args.append(nc.dram_tensor(f"in_{name}_dram", a.shape, _mybir.dt.from_np(a.dtype), kind="ExternalInput").ap())
    shape = inputs['x'].shape
    out = nc.dram_tensor("out_0_dram", shape, _mybir.dt.from_np(_np.dtype('float32')), kind="ExternalOutput").ap()
    rgcn_kernel(nc, *args, out)
    r = _run(nc, [arrays], core_ids=[0])
    return r.results[0]["out_0_dram"]
```

```python
from contextlib import ExitStack

import concourse.bass as bass
from concourse import mybir

ALU = mybir.AluOpType
ACT = mybir.ActivationFunctionType
AX = mybir.AxisListType
F32 = mybir.dt.float32
F32R = mybir.dt.float32r
I32 = mybir.dt.int32
RMAX = bass.bass_isa.ReduceOp.max

P = 128
LN_EPS = 1e-5
RATE = 0.1


def rgcn_kernel(nc, x, src, dst, edge_type, edge_time, basis1, comp1, loop_w1, bias1,
                basis2, comp2, loop_w2, bias2, ln_g, ln_b, current_time, out):
    N, D = x.shape
    E = src.shape[0]
    R, B = comp1.shape
    KH = D // P
    ET = -(-E // P)
    FULL = E // ET
    REST = E - FULL * ET
    TG = 4
    GR = TG * P
    NG = -(-N // GR)
    NQ = NG * TG // 2
    W2 = 2 * D
    NBK = B * D // W2
    CH = 2 * (NBK - 1)
    TA = 8
    TE = 4
    XS = 4
    ROW_PARTS = 8
    assert KH == 2 and W2 == 512 and B == 2 * NBK and NG % 2 == 0 and ET % 2 == 0
    assert FULL == P - 1 and E - FULL * ET > 0

    pre1 = nc.dram_tensor("pre1", (N + P, D), F32, kind="Internal").ap()
    agg2 = nc.dram_tensor("agg2", (N + P, D), F32, kind="Internal").ap()

    def base(g):
        return N - GR if isinstance(g, int) and g == NG - 1 else g * GR

    def rows(t, g):
        return t[bass.ds(base(g), GR), :].rearrange("(p j) d -> p (j d)", p=P)

    with ExitStack() as ctx:
        def sb(name, shape, dt=F32):
            return ctx.enter_context(nc.sbuf_tensor(name, shape, dt))

        def sem(name):
            return ctx.enter_context(nc.semaphore(name))

        ident = sb("ident", [P, P])
        tril = sb("tril", [P, P])
        ones_rows = sb("ones_rows", [P, P], F32R)
        bias_rows = sb("bias_rows", [P, W2], F32R)
        bias_raw = sb("bias_raw", [2, D])
        bias_hi = sb("bias_hi", [2, D])
        bias_hr = sb("bias_hr", [2, D], F32R)
        bias_lo = sb("bias_lo", [2, D])
        agg_init = sb("agg_init", [P, TG, D])
        zero_row = sb("zero_row", [P, D])
        g_bc = sb("g_bc", [P, 2, D])
        b_bc = sb("b_bc", [P, 2, D])
        eps = sb("eps", [P, 1])
        basis_raw = sb("basis_raw", [P, KH, B * D])
        basis_hi = sb("basis_hi", [P, KH, B * D], F32R)
        basis_lo = sb("basis_lo", [P, KH, B * D], F32R)
        loop_raw = sb("loop_raw", [P, 2, KH, D])
        loop_hi = sb("loop_hi", [P, 2, KH, D], F32R)
        loop_lo = sb("loop_lo", [P, 2, KH, D], F32R)
        src_i = sb("src_i", [P, ET], I32)
        type_i = sb("type_i", [P, ET], I32)
        dst_i = sb("dst_i", [P, ET], I32)
        src_type = sb("src_type", [P, ET, 2], I32)
        dst_f = sb("dst_f", [P, ET])
        spare = sb("spare", [P, ET])
        dst_row = sb("dst_row", [P, P, ET], I32)
        etime = sb("etime", [P, ET])
        ctime = sb("ctime", [P, 1])
        decay = sb("decay", [P, ET])
        tmax = sb("tmax", [P, 4])
        rstd = sb("rstd", [P, NG * TG])
        nmr = sb("nmr", [P, NG * TG])
        xg = sb("xg", [P, XS, TG * D])
        zg = sb("zg", [P, 2, TG * D])
        og = sb("og", [P, 2, TG * D])
        ag = sb("ag", [P, 2, TG * D])
        hi = sb("hi", [P, 2, W2], F32R)
        lo = sb("lo", [P, 2, W2], F32R)
        st = sb("st", [P, 4, 6])
        mv = sb("mv", [P, 2, TG, 2])
        std = sb("std", [P, 2, TG])
        xe = sb("xe", [P, TE, D])
        ids = sb("ids", [P, TE, 2], I32)
        cr = sb("cr", [P, TE, B])
        cw = sb("cw", [P, 2, B])
        acc = ag[:, 0].rearrange("p (s j d) -> p s j d", s=2, j=2)
        msg = ag[:, 1, 0:2 * D].rearrange("p (s d) -> p s d", s=2)
        magg = ag[:, 1, 2 * D:4 * D].rearrange("p (s d) -> p s d", s=2)
        msg_hi = sb("msg_hi", [P, 2, D], F32R)
        msg_lo = sb("msg_lo", [P, 2, D], F32R)
        same = sb("same", [P, 2, P], F32R)
        junk = sb("junk", [P, P])
        dup = sb("dup", [P, 2])
        sidx = sb("sidx", [P, 2, 1], I32)
        est = sb("est", [P, 6])
        emv = sb("emv", [P, 2])
        estd = sb("estd", [P, 1])
        enr = sb("enr", [P, 2])
        spot = dst_row[:, :, :].rearrange("q p t -> q (p t)").bitcast(F32)

        def carve(at, n):
            return spot[:, at * W2:(at + n) * W2].rearrange("p (s w) -> p s w", w=W2)

        h0, v, y, yg, xb = carve(0, 2), carve(2, 4), carve(6, 2), carve(8, 4), carve(12, 4)
        cst = sb("cst", [P, 2, 6])
        cmv = sb("cmv", [P, 2, 2, 2])
        cstd = sb("cstd", [P, 2, 2])
        cnr = sb("cnr", [P, 2, 2, 2])

        psT = [ctx.enter_context(nc.psum_tensor(f"psT{i}", [P, W2], F32)) for i in range(2)]
        psM = [ctx.enter_context(nc.psum_tensor(f"psM{i}", [P, W2], F32)) for i in range(NBK)]
        psS = ctx.enter_context(nc.psum_tensor("psS", [P, W2], F32))

        s_w = sem("s_w")
        s_pool_go = sem("s_pool_go")
        s_dve_go = sem("s_dve_go")
        s_small = sem("s_small")
        s_edges = sem("s_edges")
        s_dst_row = sem("s_dst_row")
        s_clear = sem("s_clear")
        s_const = sem("s_const")
        s_pool = sem("s_pool")
        s_loop_hi = sem("s_loop_hi")
        s_loop_lo = sem("s_loop_lo")
        s_bias = sem("s_bias")
        s_bias_hi = sem("s_bias_hi")
        s_basis_raw = sem("s_basis_raw")
        s_basis_hi = [sem(f"s_basis_hi{l}") for l in range(2)]
        s_basis_lo = [sem(f"s_basis_lo{l}") for l in range(2)]
        s_td = sem("s_td")
        s_tmax = sem("s_tmax")
        s_exp = sem("s_exp")
        s_dst = sem("s_dst")
        s_dummy = sem("s_dummy")
        s_agg_init = sem("s_agg_init")
        s_agg = sem("s_agg")
        a_x = [sem(f"a_x{i}") for i in range(XS)]
        a_st = sem("a_st")
        a_mv = sem("a_mv")
        a_std = sem("a_std")
        a_rstd = sem("a_rstd")
        a_nmr = sem("a_nmr")
        a_zd = sem("a_zd")
        a_za = sem("a_za")
        a_tr = sem("a_tr")
        a_hi = sem("a_hi")
        a_lo = sem("a_lo")
        a_mm = sem("a_mm")
        a_ev = sem("a_ev")
        a_out = [sem(f"a_out{i}") for i in range(2)]
        names = ["ids", "stat", "mv", "std", "rstd", "nmr", "z", "tr", "hi", "lo", "mm", "cw", "init", "comb",
                 "msg", "mhi", "mlo", "same", "dup", "dupc", "sidx", "smm", "magg", "scat"]
        e = [{n: sem(f"e{l}_{n}") for n in names} for l in range(2)]
        for l in range(2):
            e[l]["row"] = [sem(f"e{l}_row{i}") for i in range(TE)]
            e[l]["coef"] = [sem(f"e{l}_coef{i}") for i in range(TE)]
        c_p = [sem(f"c_p{i}") for i in range(2)]
        c_x = [sem(f"c_x{i}") for i in range(XS)]
        c_a = [sem(f"c_a{i}") for i in range(2)]
        c_out = [sem(f"c_out{i}") for i in range(2)]
        c_tr = sem("c_tr")
        c_hi = sem("c_hi")
        c_lo = sem("c_lo")
        c_mm = sem("c_mm")
        c_h0 = sem("c_h0")
        c_v = sem("c_v")
        c_st = sem("c_st")
        c_mv = sem("c_mv")
        c_std = sem("c_std")
        c_rstd = sem("c_rstd")
        c_nmr = sem("c_nmr")
        c_y = sem("c_y")
        c_yg = sem("c_yg")
        c_xb = sem("c_xb")
        c_o = sem("c_o")

        def after(eng, s, count):
            if not isinstance(count, int) or count > 0:
                eng.wait_ge(s, count)

        def ran(i, n):
            return not isinstance(i, int) or 0 <= i < n

        def looped(eng, first, trips, late, body):
            for it in range(first, 1):
                body(it)
            with eng.Fori(1, trips - late) as it:
                body(it)
            for it in range(trips - late, trips):
                body(it)

        def node_loop(eng, body):
            looped(eng, -1, NQ // TA + 2, 3, body)

        def edge_loop(eng, body):
            looped(eng, -1, ET // TE + 1, 2, body)

        block = ctx.enter_context(nc.Block())

        def flat(v):
            return v.rearrange("(a n) -> a n", a=1)

        @block.sync
        def _(sp):
            sp.dma_start(loop_raw[:, 0], loop_w1.rearrange("(k p) n -> p k n", p=P)).then_inc(s_w, 16)
            sp.dma_start(loop_raw[:, 1], loop_w2.rearrange("(k p) n -> p k n", p=P)).then_inc(s_w, 16)
            for r in range(2):
                sp.dma_start(bias_raw[r:r + 1, :], flat(bias1)).then_inc(s_small, 16)
            sp.dma_start(ctime[:, :], flat(current_time).to_broadcast([P, 1])).then_inc(s_small, 16)
            for j in range(2):
                sp.dma_start(g_bc[:, j, :], flat(ln_g).to_broadcast([P, D])).then_inc(s_small, 16)
                sp.dma_start(b_bc[:, j, :], flat(ln_b).to_broadcast([P, D])).then_inc(s_small, 16)

            def load_x(it):
                for k in range(XS):
                    g = XS * it + k
                    if not ran(g, NG):
                        continue
                    after(sp, a_zd, 2 * g - 2 * XS + 2)
                    after(sp, a_za, 2 * g - 2 * XS + 2)
                    sp.dma_start(xg[:, k], rows(x, g)).then_inc(a_x[k], 16)

            def load_lists():
                for j in range(TG):
                    sp.dma_start(agg_init[:, j, :], flat(bias2).to_broadcast([P, D])).then_inc(s_agg_init, 16)
                sp.wait_ge(s_clear, 5)
                for t, v in ((src_i, src), (type_i, edge_type), (dst_i, dst), (etime, edge_time)):
                    sp.dma_start(t[0:FULL, :], v[0:FULL * ET].rearrange("(p t) -> p t", t=ET)).then_inc(s_edges, 16)
                    sp.dma_start(t[FULL:P, 0:REST], flat(v[FULL * ET:E])).then_inc(s_edges, 16)

            def load_dst_row(part):
                a, b = part * E // ROW_PARTS, (part + 1) * E // ROW_PARTS
                sp.dma_start(dst_row[:, :, :].rearrange("q p t -> q (p t)")[:, a:b],
                             flat(dst)[:, a:b].to_broadcast([P, b - a])).then_inc(s_dst_row, 16)

            def load_basis(basis):
                for kh in range(KH):
                    sp.dma_start(basis_raw[:, kh], basis[:, kh * P:(kh + 1) * P, :].rearrange("b p n -> p b n")
                                 ).then_inc(s_basis_raw, 16)

            load_x(0)
            load_lists()
            with sp.Fori(1, 5) as it:
                load_x(it)
            load_basis(basis1)
            for it in range(5, 5 + ROW_PARTS):
                load_x(it)
                load_dst_row(it - 5)
            with sp.Fori(5 + ROW_PARTS, NG // XS) as it:
                load_x(it)
            load_x(NG // XS)

            sp.wait_ge(s_agg_init, 16 * TG)

            with sp.Fori(0, NG - 1) as g:
                sp.wait_ge(e[0]["hi"], g + 1)
                sp.dma_start(rows(agg2, g), agg_init[:, :, :].rearrange("p j d -> p (j d)")).then_inc(s_agg, 16)
            sp.wait_ge(s_agg, 16 * (NG - 1))
            sp.dma_start(rows(agg2, NG - 1), agg_init[:, :, :].rearrange("p j d -> p (j d)")).then_inc(s_agg, 16)

            sp.wait_ge(s_basis_hi[0], KH)
            sp.wait_ge(s_basis_lo[0], KH)
            load_basis(basis2)

            def load_c(it):
                for k in range(XS):
                    g = XS * it + k
                    if not ran(g, NG):
                        continue
                    s = k % 2
                    after(sp, c_tr, 2 * g - 2)
                    sp.dma_start(zg[:, s], rows(pre1, g)).then_inc(c_p[s], 16)
                    after(sp, c_xb, 2 * g - 2 * XS + 2)
                    after(sp, c_h0, 2 * g - 2 * XS + 2)
                    sp.dma_start(xg[:, k], rows(x, g)).then_inc(c_x[k], 16)
                    if isinstance(g, int) and g == 0:
                        sp.wait_ge(e[1]["scat"], 16 * ET)
                    after(sp, c_mm, 2 * g - 2)
                    sp.dma_start(ag[:, s], rows(agg2, g)).then_inc(c_a[s], 16)

            sp.wait_ge(e[0]["scat"], 16 * ET)
            load_c(0)
            with sp.Fori(1, NG // XS) as it:
                load_c(it)
            load_c(NG // XS)
            sp.wait_ge(c_out[0], 16 * (NG // 2))
            sp.wait_ge(c_out[1], 16 * (NG // 2))

        @block.gpsimd
        def _(pool):
            pool.memset(ident[:], 0.0).then_inc(s_pool, 1)
            pool.memset(tril[:], 1.0).then_inc(s_pool, 1)
            pool.memset(ones_rows[:].bitcast(F32), 0.0).then_inc(s_pool, 1)
            pool.wait_ge(s_pool, 3)
            pool.affine_select(out=ident[:], in_=ident[:], compare_op=ALU.not_equal, fill=1.0, base=0,
                               pattern=[[-1, P]], channel_multiplier=1).then_inc(s_const, 1)
            pool.affine_select(out=tril[:], in_=tril[:], compare_op=ALU.is_gt, fill=0.0, base=0,
                               pattern=[[-1, P]], channel_multiplier=1).then_inc(s_const, 1)
            pool.memset(ones_rows[0:2, :].bitcast(F32), 1.0).then_inc(s_const, 1)
            pool.memset(eps[:], LN_EPS).then_inc(s_const, 1)
            pool.memset(bias_rows[:].bitcast(F32), 0.0).then_inc(s_const, 1)
            pool.memset(src_i[:], 0).then_inc(s_clear, 1)
            pool.memset(type_i[:], 0).then_inc(s_clear, 1)
            pool.memset(dst_i[:], N + P - 1).then_inc(s_clear, 1)
            pool.memset(etime[:], 3.0e38).then_inc(s_clear, 1)
            pool.memset(dst_row[:, FULL, :], N + P - 1).then_inc(s_clear, 1)
            pool.memset(zero_row[:], 0.0).then_inc(s_dst, 1)
            pool.iota(spare[:], pattern=[[0, ET]], base=N, channel_multiplier=1,
                      allow_small_or_imprecise_dtypes=True).then_inc(s_dst, 1)
            pool.wait_ge(s_dst, 1)
            for t in (pre1, agg2):
                pool.dma_start(t[N:N + P, :], zero_row[:]).then_inc(s_dummy, 16)
            pool.wait_ge(s_edges, 16 * 8)
            pool.tensor_copy(src_type[:, :, 0], src_i[:]).then_inc(s_pool, 1)
            pool.tensor_copy(src_type[:, :, 1], type_i[:]).then_inc(s_pool, 1)
            pool.wait_ge(s_pool, 5)
            pool.wait_ge(s_td, 3)
            pool.partition_all_reduce(tmax[:, 1:2], tmax[:, 0:1], P, RMAX).then_inc(s_tmax, 1)

            for l in range(2):
                el = e[l]
                table = x if l == 0 else pre1
                comp = comp1 if l == 0 else comp2
                target = pre1 if l == 0 else agg2
                if l == 0:
                    pool.wait_ge(s_dummy, 32)
                else:
                    pool.wait_ge(e[0]["scat"], 16 * ET)
                    pool.wait_ge(e[0]["cw"], ET)
                    pool.wait_ge(e[0]["tr"], ET)

                def gather(t, s, turn):
                    after(pool, el["row"][s], 16 * turn)
                    after(pool, el["coef"][s], 16 * turn)
                    pool.tensor_copy(ids[:, s], src_type[:, bass.ds(t, 1), :].rearrange("p a b -> p (a b)")).then_inc(el["ids"], 1)
                    pool.wait_ge(el["ids"], t + 1)
                    after(pool, el["tr"], t - TE + 1)
                    pool.sem_inc(s_pool_go, 1)
                    pool.indirect_dma_start(out=xe[:, s], out_offset=None, in_=table[:, :],
                                            in_offset=bass.IndirectOffsetOnAxis(ap=ids[:, s, 0:1], axis=0)
                                            ).then_inc(el["row"][s], 16)
                    after(pool, el["cw"], t - TE + 1)
                    pool.sem_inc(s_pool_go, 1)
                    pool.indirect_dma_start(out=cr[:, s], out_offset=None, in_=comp[:, :],
                                            in_offset=bass.IndirectOffsetOnAxis(ap=ids[:, s, 1:2], axis=0)
                                            ).then_inc(el["coef"][s], 16)

                def scatter(t, s):
                    after(pool, el["scat"], 16 * t)
                    if l == 0 and isinstance(t, int) and t == 0:
                        pool.wait_ge(a_out[0], 16 * (NG // 2))
                        pool.wait_ge(a_out[1], 16 * (NG // 2))
                    if l == 1 and isinstance(t, int) and t == 0:
                        pool.wait_ge(s_agg, 16 * NG)
                    pool.wait_ge(el["magg"], t + 1)
                    pool.wait_ge(el["sidx"], t + 1)
                    pool.sem_inc(s_pool_go, 1)
                    pool.indirect_dma_start(out=target[:, :],
                                            out_offset=bass.IndirectOffsetOnAxis(ap=sidx[:, s, :], axis=0),
                                            in_=magg[:, s], in_offset=None, compute_op=ALU.add
                                            ).then_inc(el["scat"], 16)

                def edges(it):
                    for k in range(TE):
                        t = TE * it + k
                        if ran(t + 3, ET):
                            gather(t + 3, (k + 3) % TE, it + (k + 3) // TE)
                        if ran(t - 1, ET):
                            scatter(t - 1, (k - 1) % 2)

                edge_loop(pool, edges)

            def nodes_c(it):
                for k in range(TA):
                    q = TA * it + k - 3
                    if ran(q, NQ):
                        h = (k - 3) % 2
                        if h == 0:
                            pool.wait_ge(c_x[(k - 3) // 2 % XS], 16 * (it + 1 + (k - 3) // TA))
                        after(pool, c_o, q - 3)
                        pool.tensor_tensor(xb[:, (k - 3) % 4], xg[:, (k - 3) // 2 % XS, h * W2:(h + 1) * W2],
                                           b_bc[:, :, :].rearrange("p j d -> p (j d)"), ALU.add).then_inc(c_xb, 1)
                        pool.wait_ge(c_y, q + 1)
                        pool.tensor_tensor(yg[:, (k - 3) % 4], y[:, h],
                                           g_bc[:, :, :].rearrange("p j d -> p (j d)"), ALU.mult).then_inc(c_yg, 1)

            node_loop(pool, nodes_c)

        @block.tensor
        def _(pe):
            pe.wait_ge(s_const, 5)
            pe.wait_ge(s_bias, 2)
            pe.wait_ge(s_loop_hi, 1)
            pe.wait_ge(s_loop_lo, 1)

            def transposes(bank, tile, done):
                n = tile.shape[1] // P
                for i in range(n):
                    last = pe.transpose(psT[bank][:, i * P:(i + 1) * P], tile[:, i * P:(i + 1) * P], ident[:])
                last.then_inc(done, 1)

            def node_products(layer, b, done):
                for j in range(2):
                    o = psM[b][:, j * D:(j + 1) * D]
                    for kh in range(KH):
                        c = (j * KH + kh) * P
                        for h, w in ((hi, loop_hi), (hi, loop_lo), (lo, loop_hi)):
                            last = pe.matmul(o, h[:, b, c:c + P], w[:, layer, kh, :], start=False,
                                             stop=(j == 1 and kh == KH - 1 and h is lo), skip_group_check=True)
                last.then_inc(done, 1)

            def nodes_a(it):
                for k in range(TA):
                    q = TA * it + k
                    if ran(q + 1, NQ):
                        pe.wait_ge(a_zd, q + 2)
                        pe.wait_ge(a_za, q + 2)
                        after(pe, a_hi, q)
                        after(pe, a_lo, q)
                        h = (k + 1) % 2
                        transposes(h, zg[:, (k + 1) // 2 % 2, h * W2:(h + 1) * W2], a_tr)
                    if ran(q, NQ):
                        after(pe, a_ev, q - 1)
                        pe.wait_ge(a_hi, q + 1)
                        pe.wait_ge(a_lo, q + 1)
                        pe.matmul(psM[k % 2][:], ones_rows[:], bias_rows[:], start=True, stop=False, skip_group_check=True)
                        node_products(0, k % 2, a_mm)

            def nodes_c(it):
                for k in range(TA):
                    q = TA * it + k
                    if ran(q + 1, NQ):
                        h, s = (k + 1) % 2, (k + 1) // 2 % 2
                        if h == 0:
                            pe.wait_ge(c_p[s], 16 * (2 * it + (k + 1) // 4 + 1))
                        after(pe, c_hi, q)
                        after(pe, c_lo, q)
                        transposes(h, zg[:, s, h * W2:(h + 1) * W2], c_tr)
                    if ran(q, NQ):
                        h, s = k % 2, k // 2 % 2
                        if h == 0:
                            pe.wait_ge(c_a[s], 16 * (2 * it + k // 4 + 1))
                        after(pe, c_v, q - 1)
                        pe.matmul(psM[h][:], ident[:], ag[:, s, h * W2:(h + 1) * W2], start=True, stop=False,
                                  skip_group_check=True)
                        pe.wait_ge(c_hi, q + 1)
                        pe.wait_ge(c_lo, q + 1)
                        node_products(1, h, c_mm)

            node_loop(pe, nodes_a)

            for l in range(2):
                el = e[l]

                def transpose_edges(t, s, turn):
                    if l == 0:
                        pe.wait_ge(el["z"], t + 1)
                    else:
                        pe.wait_ge(el["row"][s], 16 * (turn + 1))
                    transposes(s % 2, xe[:, s], el["tr"])

                def combine_duplicates(t, s):
                    pe.wait_ge(el["same"], t + 1)
                    pe.wait_ge(el["mhi"], t + 1)
                    after(pe, el["magg"], t)
                    pe.matmul(psS[:, 0:D], same[:, s], msg_hi[:, s], start=True, stop=False)
                    pe.wait_ge(el["mlo"], t + 1)
                    pe.matmul(psS[:, 0:D], same[:, s], msg_lo[:, s], start=False, stop=True).then_inc(el["smm"], 1)

                if l == 0:
                    pe.wait_ge(a_ev, NQ)
                else:
                    pe.wait_ge(e[0]["magg"], ET)

                def edges(it):
                    for k in range(TE):
                        t = TE * it + k
                        for b in range(NBK):
                            if ran(t, ET):
                                if b == 0:
                                    if isinstance(t, int) and t == 0:
                                        pe.wait_ge(s_basis_hi[l], KH)
                                        pe.wait_ge(s_basis_lo[l], KH)
                                    pe.wait_ge(el["hi"], t + 1)
                                    pe.wait_ge(el["lo"], t + 1)
                                    after(pe, el["init"], 2 * t)
                                else:
                                    after(pe, el["comb"], CH * (t - 1) + 2 * b)
                                n = 0
                                for kh in range(KH):
                                    for h, w in ((hi, basis_hi), (hi, basis_lo), (lo, basis_hi)):
                                        last = pe.matmul(psM[b][:], h[:, k % 2, kh * P:(kh + 1) * P],
                                                         w[:, kh, b * W2:(b + 1) * W2], start=(n == 0), stop=(n == 3 * KH - 1))
                                        n += 1
                                last.then_inc(el["mm"], 1)
                            if b == 1 and ran(t + 1, ET):
                                transpose_edges(t + 1, (k + 1) % TE, it + (k + 1) // TE)
                            if b == 3 and ran(t - 1, ET):
                                combine_duplicates(t - 1, (k - 1) % 2)

                edge_loop(pe, edges)

            pe.wait_ge(e[1]["magg"], ET)
            node_loop(pe, nodes_c)

        @block.scalar
        def _(act):
            act.wait_ge(s_w, 32)
            act.activation(loop_hi[:], loop_raw[:], ACT.Copy).then_inc(s_loop_hi, 1)
            act.wait_ge(s_small, 16 * 7)
            act.activation(bias_hr[:], bias_raw[:], ACT.Copy).then_inc(s_bias_hi, 1)
            act.wait_ge(s_const, 5)

            def split_hi(s, w, done):
                act.activation(hi[:, s, 0:w], psT[s][:, 0:w], ACT.Relu).then_inc(done, 1)

            def nodes_a(it):
                for k in range(TA):
                    q = TA * it + k
                    if ran(q - 1, NQ):
                        h, s = (k - 1) % 2, (k - 1) // 2 % 2
                        if h == 0:
                            after(act, a_out[s], 16 * (2 * it + (k - 1) // 4))
                        act.wait_ge(a_mm, q)
                        act.activation(og[:, s, h * W2:(h + 1) * W2], psM[h][:], ACT.Copy).then_inc(a_ev, 1)
                    if ran(q + 1, NQ):
                        act.wait_ge(a_tr, q + 2)
                        after(act, a_mm, q)
                        split_hi((k + 1) % 2, W2, a_hi)
                    if ran(q + 2, NQ):
                        act.wait_ge(a_nmr, 4 * it + (k + 2) // 2 + 1)
                        after(act, a_tr, q - 1)
                        h, s = k % 2, (k + 2) // 2
                        o = h * W2 + D
                        c = bass.ds(4 * TG * it + TG * s + 2 * h + 1, 1)
                        act.activation(zg[:, s % 2, o:o + D], xg[:, s % XS, o:o + D], ACT.Identity,
                                       bias=nmr[:, c], scale=rstd[:, c]).then_inc(a_za, 1)
                    if k % 2 == 0 and ran(4 * it + k // 2 + 2, NG):
                        g = 4 * it + k // 2 + 2
                        act.wait_ge(a_mv, g + 1)
                        after(act, a_rstd, g - 1)
                        act.activation(std[:, k // 2 % 2], mv[:, k // 2 % 2, :, 1], ACT.Sqrt, bias=eps[:]).then_inc(a_std, 1)
                    if k % 2 == 0 and ran(4 * it + k // 2 - 1, NG):
                        g = 4 * it + k // 2 - 1
                        s = (k // 2 - 1) % 2
                        act.wait_ge(a_ev, 2 * g + 2)
                        if isinstance(g, int) and g == NG - 1:
                            act.wait_ge(a_out[0], 16 * (NG // 2))
                        act.dma_start(rows(pre1, g), og[:, s]).then_inc(a_out[s], 16)

            def decay_edges():
                act.wait_ge(s_td, 6)
                act.activation(decay[:], etime[:], ACT.Exp, scale=-RATE).then_inc(s_exp, 1)

            def split_basis(l):
                for kh in range(KH):
                    act.activation(basis_hi[:, kh], basis_raw[:, kh], ACT.Copy).then_inc(s_basis_hi[l], 1)

            nodes_a(-1)
            nodes_a(0)
            with act.Fori(1, NQ // TA - 1) as it:
                nodes_a(it)
            decay_edges()
            act.wait_ge(s_basis_raw, 16 * KH)
            split_basis(0)
            nodes_a(NQ // TA - 1)
            nodes_a(NQ // TA)

            for l in range(2):
                el = e[l]

                def std_e(t):
                    act.wait_ge(el["mv"], t + 1)
                    act.activation(estd[:], emv[:, 1:2], ACT.Sqrt, bias=eps[:]).then_inc(el["std"], 1)

                def start_e(t, s):
                    act.wait_ge(el["cw"], t + 1)
                    after(act, el["msg"], t - 1)
                    act.wait_ge(el["mm"], NBK * t + 1)
                    for j in range(2):
                        act.activation(acc[:, s, j], psM[0][:, j * D:(j + 1) * D], ACT.Copy, scale=cw[:, s, j:j + 1]
                                       ).then_inc(el["init"], 1)

                def hi_e(t, s):
                    act.wait_ge(el["tr"], t + 1)
                    after(act, el["mm"], NBK * (t - 1))
                    split_hi(s, D, el["hi"])

                def magg_e(t, s):
                    act.wait_ge(el["smm"], t + 1)
                    after(act, el["scat"], 16 * (t - 1))
                    act.activation(magg[:, s], psS[:, 0:D], ACT.Copy).then_inc(el["magg"], 1)

                if l == 1:
                    act.wait_ge(s_basis_raw, 2 * 16 * KH)
                    act.wait_ge(e[0]["mm"], NBK * ET)
                    split_basis(1)

                def edges(it):
                    for k in range(TE):
                        t = TE * it + k
                        if ran(t - 1, ET):
                            s = (k - 1) % 2
                            act.wait_ge(el["msg"], t)
                            after(act, el["smm"], t - 2)
                            act.activation(msg_hi[:, s], msg[:, s], ACT.Copy).then_inc(el["mhi"], 1)
                        if ran(t, ET):
                            start_e(t, k % 2)
                        if ran(t + 1, ET):
                            hi_e(t + 1, (k + 1) % 2)
                        if l == 0 and ran(t + 2, ET):
                            std_e(t + 2)
                        if ran(t - 1, ET):
                            magg_e(t - 1, (k - 1) % 2)

                edge_loop(act, edges)

            def nodes_c(it):
                for k in range(TA):
                    q = TA * it + k

                    def h0_c(j):
                        a = k % 2 * W2 + j * D
                        c = bass.ds(2 * q + j, 1)
                        return act.activation(h0[:, k % 2, j * D:(j + 1) * D], xg[:, k // 2, a:a + D], ACT.Relu,
                                              bias=nmr[:, c], scale=rstd[:, c])

                    if ran(q - 2, NQ):
                        act.wait_ge(c_mv, q - 1)
                        after(act, c_rstd, q - 3)
                        act.activation(cstd[:, k % 2], cmv[:, k % 2, :, 1], ACT.Sqrt, bias=eps[:]).then_inc(c_std, 1)
                    if ran(q + 1, NQ):
                        act.wait_ge(c_tr, q + 2)
                        after(act, c_mm, q)
                        split_hi((k + 1) % 2, W2, c_hi)
                    if ran(q, NQ):
                        if k % 2 == 0:
                            act.wait_ge(c_x[k // 2], 16 * (it + 1))
                        after(act, c_v, q - 1)
                        h0_c(0)
                        h0_c(1).then_inc(c_h0, 1)
                    if ran(q - 3, NQ):
                        s = (k - 3) % 2
                        act.wait_ge(c_nmr, q - 2)
                        after(act, c_yg, q - 4)
                        for j in range(2):
                            last = act.activation(y[:, s, j * D:(j + 1) * D], v[:, (k - 3) % 4, j * D:(j + 1) * D],
                                                  ACT.Identity, bias=cnr[:, s, 1, j:j + 1], scale=cnr[:, s, 0, j:j + 1])
                        last.then_inc(c_y, 1)
                    if k % 2 == 1 and ran(4 * it + k // 2 - 3, NG):
                        g, s = 4 * it + k // 2 - 3, (k // 2 - 3) % 2
                        act.wait_ge(c_o, 2 * g + 2)
                        if isinstance(g, int) and g == NG - 1:
                            act.wait_ge(c_out[0], 16 * (NG // 2))
                        act.dma_start(rows(out, g), og[:, s]).then_inc(c_out[s], 16)

            node_loop(act, nodes_c)

        @block.vector
        def _(dve):
            dve.wait_ge(s_loop_hi, 1)
            dve.tensor_tensor(loop_lo[:], loop_raw[:], loop_hi[:].bitcast(F32), ALU.subtract).then_inc(s_loop_lo, 1)
            dve.wait_ge(s_bias_hi, 1)
            dve.wait_ge(s_const, 5)
            dve.tensor_tensor(bias_lo[:], bias_raw[:], bias_hr[:].bitcast(F32), ALU.subtract).then_inc(s_bias_hi, 1)
            dve.wait_ge(s_bias_hi, 2)
            dve.tensor_scalar(bias_hi[:], bias_lo[:], ident[0:2, 1:2], None, ALU.mult).then_inc(s_bias_hi, 1)
            dve.wait_ge(s_bias_hi, 3)
            for j in range(2):
                dve.scalar_tensor_tensor(out=bias_rows[0:2, j * D:(j + 1) * D], in0=bias_hr[:].bitcast(F32),
                                         scalar=ident[0:2, 0:1], in1=bias_hi[:], op0=ALU.mult, op1=ALU.add).then_inc(s_bias, 1)

            def split_lo(s, w, done):
                dve.scalar_tensor_tensor(out=lo[:, s, 0:w], in0=psT[s][:, 0:w], scalar=0.0, in1=hi[:, s, 0:w].bitcast(F32),
                                         op0=ALU.max, op1=ALU.subtract).then_inc(done, 1)

            def nodes_a(it):
                for k in range(TA):
                    q = TA * it + k
                    g = 4 * it + k // 2 + 2
                    if k % 2 == 1 and ran(g, NG):
                        c = bass.ds(g * TG, TG)
                        dve.wait_ge(a_std, g + 1)
                        dve.reciprocal(rstd[:, c], std[:, k // 2 % 2]).then_inc(a_rstd, 1)
                    if ran(q + 2, NQ):
                        h, s = k % 2, (k + 2) // 2
                        dve.wait_ge(a_nmr, 4 * it + s + 1)
                        after(dve, a_tr, q - 1)
                        o = h * W2
                        cz = bass.ds(4 * TG * it + TG * s + 2 * h, 1)
                        dve.tensor_scalar(zg[:, s % 2, o:o + D], xg[:, s % XS, o:o + D], rstd[:, cz], nmr[:, cz],
                                          ALU.mult, ALU.add).then_inc(a_zd, 1)
                    if k % 2 == 1 and ran(g, NG):
                        dve.wait_ge(a_rstd, g + 1)
                        dve.scalar_tensor_tensor(out=nmr[:, c], in0=mv[:, k // 2 % 2, :, 0], scalar=-1.0, in1=rstd[:, c],
                                                 op0=ALU.mult, op1=ALU.mult).then_inc(a_nmr, 1)
                    if k % 2 == 0 and ran(g, NG):
                        dve.wait_ge(a_st, g + 1)
                        after(dve, a_nmr, g - 1)
                        dve.sem_inc(s_dve_go, 1)
                        for j in range(TG):
                            last = dve.bn_aggr(mv[:, k // 2 % 2, j], st[:, j])
                        last.then_inc(a_mv, 1)
                    if ran(q + 1, NQ):
                        dve.wait_ge(a_hi, q + 2)
                        split_lo((k + 1) % 2, W2, a_lo)
                    g = 4 * it + k // 2 + 3
                    if ran(g, NG):
                        if k % 2 == 0:
                            dve.wait_ge(a_x[(k // 2 + 3) % XS], 16 * (it + 1 + (k // 2 + 3) // XS))
                            after(dve, a_mv, g)
                        for j in range(2 * (k % 2), 2 * (k % 2) + 2):
                            last = dve.bn_stats(st[:, j], xg[:, (k // 2 + 3) % XS, j * D:(j + 1) * D])
                        if k % 2 == 1:
                            last.then_inc(a_st, 1)

            def prepare_edges():
                dve.wait_ge(s_edges, 16 * 8)
                dve.wait_ge(s_dst_row, 16 * ROW_PARTS)
                dve.wait_ge(s_small, 16 * 7)
                dve.tensor_scalar(decay[:], etime[:], -1.0, ctime[:], ALU.mult, ALU.add).then_inc(s_td, 1)
                dve.wait_ge(s_td, 1)
                dve.tensor_scalar(decay[:], decay[:], 0.0, None, ALU.max).then_inc(s_td, 1)
                dve.wait_ge(s_td, 2)
                dve.tensor_reduce(tmax[:, 0:1], decay[:], AX.X, ALU.max).then_inc(s_td, 1)
                dve.wait_ge(s_tmax, 1)
                dve.tensor_scalar(tmax[:, 2:3], tmax[:, 1:2], 1e-8, None, ALU.add).then_inc(s_td, 1)
                dve.wait_ge(s_td, 4)
                dve.reciprocal(tmax[:, 3:4], tmax[:, 2:3]).then_inc(s_td, 1)
                dve.wait_ge(s_td, 5)
                dve.tensor_scalar(etime[:], decay[:], tmax[:, 3:4], None, ALU.mult).then_inc(s_td, 1)
                dve.wait_ge(s_dst, 2)
                dve.tensor_copy(dst_f[:], dst_i[:]).then_inc(s_td, 1)
                dve.wait_ge(s_td, 7)
                dve.tensor_tensor(spare[:], spare[:], dst_f[:], ALU.subtract).then_inc(s_td, 1)

            def split_basis(l):
                for kh in range(KH):
                    dve.wait_ge(s_basis_hi[l], kh + 1)
                    dve.tensor_tensor(basis_lo[:, kh], basis_raw[:, kh], basis_hi[:, kh].bitcast(F32),
                                      ALU.subtract).then_inc(s_basis_lo[l], 1)

            nodes_a(-1)
            nodes_a(0)
            with dve.Fori(1, NQ // TA - 1) as it:
                nodes_a(it)
            prepare_edges()
            split_basis(0)
            nodes_a(NQ // TA - 1)
            nodes_a(NQ // TA)
            dve.wait_ge(s_td, 8)
            dve.wait_ge(s_exp, 1)

            for l in range(2):
                el = e[l]

                def stats_e(t, s, turn):
                    dve.wait_ge(el["row"][s], 16 * (turn + 1))
                    after(dve, el["mv"], t)
                    dve.bn_stats(est[:], xe[:, s]).then_inc(el["stat"], 1)
                    dve.wait_ge(el["stat"], t + 1)
                    after(dve, el["nmr"], t)
                    dve.sem_inc(s_dve_go, 1)
                    dve.bn_aggr(emv[:], est[:]).then_inc(el["mv"], 1)

                def norm_e(t, s):
                    dve.wait_ge(el["std"], t + 1)
                    dve.reciprocal(enr[:, 0:1], estd[:]).then_inc(el["rstd"], 1)
                    dve.wait_ge(el["rstd"], t + 1)
                    dve.scalar_tensor_tensor(out=enr[:, 1:2], in0=emv[:, 0:1], scalar=-1.0, in1=enr[:, 0:1],
                                             op0=ALU.mult, op1=ALU.mult).then_inc(el["nmr"], 1)
                    dve.wait_ge(el["nmr"], t + 1)
                    dve.tensor_scalar(xe[:, s], xe[:, s], enr[:, 0:1], enr[:, 1:2], ALU.mult, ALU.add).then_inc(el["z"], 1)

                def lo_e(t, s):
                    dve.wait_ge(el["hi"], t + 1)
                    split_lo(s, D, el["lo"])

                if l == 1:
                    split_basis(1)

                def edges(it):
                    for k in range(TE):
                        t = TE * it + k
                        s = k % 2
                        if ran(t, ET):
                            dve.wait_ge(el["coef"][k], 16 * (it + 1))
                            after(dve, el["comb"], CH * (t - 1))
                            after(dve, el["init"], 2 * (t - 1))
                            dve.tensor_scalar(cw[:, s], cr[:, k], decay[:, bass.ds(t, 1)], None, ALU.mult).then_inc(el["cw"], 1)
                            dve.wait_ge(el["cw"], t + 1)
                        for b in range(1, NBK):
                            if ran(t, ET):
                                dve.wait_ge(el["mm"], NBK * t + b + 1)
                                for j in range(2):
                                    n = 2 * (b - 1) + j
                                    if b == 1:
                                        dve.wait_ge(el["init"], 2 * t + j + 1)
                                    else:
                                        dve.wait_ge(el["comb"], CH * t + n - 1)
                                    dve.scalar_tensor_tensor(out=acc[:, s, j], in0=psM[b][:, j * D:(j + 1) * D],
                                                             scalar=cw[:, s, n + 2:n + 3], in1=acc[:, s, j],
                                                             op0=ALU.mult, op1=ALU.add).then_inc(el["comb"], 1)
                            if b == 1 and ran(t - 1, ET):
                                dve.wait_ge(el["mhi"], t)
                                dve.tensor_tensor(msg_lo[:, 1 - s], msg[:, 1 - s], msg_hi[:, 1 - s].bitcast(F32),
                                                  ALU.subtract).then_inc(el["mlo"], 1)
                            if b == 1 and l == 0 and ran(t + 2, ET):
                                stats_e(t + 2, (k + 2) % TE, it + (k + 2) // TE)
                            if b == 2 and ran(t + 1, ET):
                                lo_e(t + 1, (k + 1) % 2)
                            if b == 3 and l == 0 and ran(t + 2, ET):
                                norm_e(t + 2, (k + 2) % TE)
                        if not ran(t, ET):
                            continue
                        after(dve, el["smm"], t - 1)
                        dve.tensor_scalar(same[:, s], dst_row[:, :, bass.ds(t, 1)].rearrange("q p t -> q (p t)"),
                                          dst_f[:, bass.ds(t, 1)], None, ALU.is_equal).then_inc(el["same"], 1)
                        dve.wait_ge(el["comb"], CH * (t + 1))
                        dve.tensor_tensor(msg[:, s], acc[:, s, 0], acc[:, s, 1], ALU.add).then_inc(el["msg"], 1)
                        dve.wait_ge(el["same"], t + 1)
                        after(dve, el["dupc"], t)
                        dve.tensor_tensor_reduce(out=junk[:], in0=same[:, s].bitcast(F32), in1=tril[:], scale=1.0, scalar=0.0,
                                                 op0=ALU.mult, op1=ALU.add, accum_out=dup[:, 0:1]).then_inc(el["dup"], 1)
                        dve.wait_ge(el["dup"], t + 1)
                        after(dve, el["sidx"], t)
                        dve.tensor_scalar(dup[:, 1:2], dup[:, 0:1], 1.0, spare[:, bass.ds(t, 1)], ALU.min, ALU.mult
                                          ).then_inc(el["dupc"], 1)
                        dve.wait_ge(el["dupc"], t + 1)
                        after(dve, el["scat"], 16 * (t - 1))
                        dve.tensor_tensor(sidx[:, s], dup[:, 1:2], dst_f[:, bass.ds(t, 1)], ALU.add).then_inc(el["sidx"], 1)

                edge_loop(dve, edges)

            def nodes_c(it):
                for k in range(TA):
                    q = TA * it + k
                    if ran(q - 1, NQ):
                        dve.wait_ge(c_h0, q)
                        after(dve, c_y, q - 4)
                        dve.wait_ge(c_mm, q)
                        dve.scalar_tensor_tensor(out=v[:, (k - 1) % 4], in0=psM[(k - 1) % 2][:], scalar=0.0,
                                                 in1=h0[:, (k - 1) % 2], op0=ALU.max, op1=ALU.add).then_inc(c_v, 1)
                    if ran(q - 2, NQ):
                        b = k % 2
                        dve.wait_ge(c_std, q - 1)
                        after(dve, c_y, q - 3)
                        dve.reciprocal(cnr[:, b, 0], cstd[:, b]).then_inc(c_rstd, 1)
                    if ran(q + 1, NQ):
                        dve.wait_ge(c_hi, q + 2)
                        split_lo((k + 1) % 2, W2, c_lo)
                    if ran(q - 2, NQ):
                        dve.wait_ge(c_rstd, q - 1)
                        dve.scalar_tensor_tensor(out=cnr[:, b, 1], in0=cmv[:, b, :, 0], scalar=-1.0, in1=cnr[:, b, 0],
                                                 op0=ALU.mult, op1=ALU.mult).then_inc(c_nmr, 1)
                    if ran(q - 1, NQ):
                        dve.wait_ge(c_v, q)
                        after(dve, c_mv, q - 1)
                        for j in range(2):
                            last = dve.bn_stats(cst[:, j], v[:, (k - 1) % 4, j * D:(j + 1) * D])
                        last.then_inc(c_st, 1)
                    if ran(q - 5, NQ):
                        h, s = (k - 5) % 2, (k - 5) // 2 % 2
                        if h == 0:
                            after(dve, c_out[s], 16 * (2 * it + (k - 5) // 4))
                        dve.wait_ge(c_xb, q - 4)
                        dve.wait_ge(c_yg, q - 4)
                        dve.tensor_tensor(og[:, s, h * W2:(h + 1) * W2], yg[:, (k - 5) % 4], xb[:, (k - 5) % 4],
                                          ALU.add).then_inc(c_o, 1)
                    if ran(q - 1, NQ):
                        dve.wait_ge(c_st, q)
                        after(dve, c_nmr, q - 2)
                        dve.sem_inc(s_dve_go, 1)
                        for j in range(2):
                            last = dve.bn_aggr(cmv[:, (k - 1) % 2, j], cst[:, j])
                        last.then_inc(c_mv, 1)

            node_loop(dve, nodes_c)


_INS = ['x', 'src', 'dst', 'edge_type_240', 'edge_weight', 'L0_gnn_basis1', 'L0_gnn_comp1', 'L0_gnn_loop_w1',
        'L0_gnn_bias1', 'L0_gnn_basis2', 'L0_gnn_comp2', 'L0_gnn_loop_w2', 'L0_gnn_bias2', 'L0_gnn_ln_g',
        'L0_gnn_ln_b', 'L0_gnn_current_time']


def kernel(**inputs):
    import numpy as _np
    import concourse.bacc as _bacc
    from concourse import mybir as _mybir
    from concourse.bass_utils import run_bass_kernel_spmd as _run

    nc = _bacc.Bacc("TRN2", target_bir_lowering=False, num_devices=1)
    arrays, args = {}, []
    for name in _INS:
        a = _np.ascontiguousarray(inputs[name])
        if a.ndim == 0:
            a = a.reshape(1)
        arrays[f"in_{name}_dram"] = a
        args.append(nc.dram_tensor(f"in_{name}_dram", a.shape, _mybir.dt.from_np(a.dtype), kind="ExternalInput").ap())
    shape = inputs['x'].shape
    out = nc.dram_tensor("out_0_dram", shape, _mybir.dt.from_np(_np.dtype('float32')), kind="ExternalOutput").ap()
    rgcn_kernel(nc, *args, out)
    r = _run(nc, [arrays], core_ids=[0])
    return r.results[0]["out_0_dram"]
```

```python
from contextlib import ExitStack

import concourse.bass as bass
from concourse import mybir

ALU = mybir.AluOpType
ACT = mybir.ActivationFunctionType
AX = mybir.AxisListType
F32 = mybir.dt.float32
F32R = mybir.dt.float32r
I32 = mybir.dt.int32
RMAX = bass.bass_isa.ReduceOp.max

P = 128
LN_EPS = 1e-5
RATE = 0.1


def rgcn_kernel(nc, x, src, dst, edge_type, edge_time, basis1, comp1, loop_w1, bias1,
                basis2, comp2, loop_w2, bias2, ln_g, ln_b, current_time, out):
    N, D = x.shape
    E = src.shape[0]
    R, B = comp1.shape
    KH = D // P
    ET = -(-E // P)
    FULL = E // ET
    REST = E - FULL * ET
    TG = 4
    GR = TG * P
    NG = -(-N // GR)
    NEW = (N - (NG - 1) * GR) // TG
    NQ = NG * TG // 2
    W2 = 2 * D
    NBK = B * D // W2
    assert NBK == 5
    CH = 2 * (NBK - 1)
    TA = 8
    TE = 4
    XS = 4
    LATE = KH * NBK
    ROW_PARTS = 10
    assert KH == 2 and W2 == 512 and B == 2 * NBK and NG % 2 == 0 and ET % 2 == 0
    assert (N - (NG - 1) * GR) % TG == 0
    assert E % ROW_PARTS == 0 and NQ // TA - 2 > LATE + KH * NBK and NG // XS > LATE + ROW_PARTS
    assert FULL == P - 1 and E - FULL * ET > 0

    pre1 = nc.dram_tensor("pre1", (N + P, D), F32, kind="Internal").ap()
    agg2 = nc.dram_tensor("agg2", (N + P, D), F32, kind="Internal").ap()

    def base(g):
        return N - GR if isinstance(g, int) and g == NG - 1 else g * GR

    def rows(t, g):
        return t[bass.ds(base(g), GR), :].rearrange("(p j) d -> p (j d)", p=P)

    def new_rows(t):
        return rows(t, NG - 1)[P - NEW:P, :]

    with ExitStack() as ctx:
        def sb(name, shape, dt=F32):
            return ctx.enter_context(nc.sbuf_tensor(name, shape, dt))

        def sem(name):
            return ctx.enter_context(nc.semaphore(name))

        ident = sb("ident", [P, P])
        tril = sb("tril", [P, P])
        bias1_bc = sb("bias1_bc", [P, 2, D])
        agg_init = sb("agg_init", [P, TG, D])
        zero_row = sb("zero_row", [P, D])
        g_bc = sb("g_bc", [P, 2, D])
        b_bc = sb("b_bc", [P, 2, D])
        eps = sb("eps", [P, 1])
        basis_raw = sb("basis_raw", [P, KH, B * D])
        basis_hi = sb("basis_hi", [P, KH, B * D], F32R)
        basis_lo = sb("basis_lo", [P, KH, B * D], F32R)
        loop_raw = sb("loop_raw", [P, 2, KH, D])
        loop_hi = sb("loop_hi", [P, 2, KH, D], F32R)
        loop_lo = sb("loop_lo", [P, 2, KH, D], F32R)
        src_i = sb("src_i", [P, ET], I32)
        type_i = sb("type_i", [P, ET], I32)
        dst_i = sb("dst_i", [P, ET], I32)
        src_type = sb("src_type", [P, ET, 2], I32)
        dst_f = sb("dst_f", [P, ET])
        spare = sb("spare", [P, ET])
        dst_row = sb("dst_row", [P, P, ET], I32)
        etime = sb("etime", [P, ET])
        ctime = sb("ctime", [P, 1])
        decay = sb("decay", [P, ET])
        tmax = sb("tmax", [P, 4])
        rstd = sb("rstd", [P, NG * TG])
        nmr = sb("nmr", [P, NG * TG])
        xg = sb("xg", [P, XS, TG * D])
        zg = sb("zg", [P, 2, TG * D])
        og = sb("og", [P, 2, TG * D])
        ag = sb("ag", [P, 2, TG * D])
        hi = sb("hi", [P, 2, W2], F32R)
        lo = sb("lo", [P, 2, W2], F32R)
        st = sb("st", [P, 4, 6])
        mv = sb("mv", [P, 2, TG, 2])
        std = sb("std", [P, 2, TG])
        xe = sb("xe", [P, TE, D])
        ids = sb("ids", [P, TE, 2], I32)
        cr = sb("cr", [P, TE, B])
        cw = sb("cw", [P, 2, B])
        acc = ag[:, 0].rearrange("p (s j d) -> p s j d", s=2, j=2)
        msg = ag[:, 1, 0:2 * D].rearrange("p (s d) -> p s d", s=2)
        magg = ag[:, 1, 2 * D:4 * D].rearrange("p (s d) -> p s d", s=2)
        msg_hi = sb("msg_hi", [P, 2, D], F32R)
        msg_lo = sb("msg_lo", [P, 2, D], F32R)
        same = sb("same", [P, 2, P], F32R)
        junk = sb("junk", [P, P])
        dup = sb("dup", [P, 2])
        sidx = sb("sidx", [P, 2, 1], I32)
        est = sb("est", [P, 6])
        emv = sb("emv", [P, 2])
        estd = sb("estd", [P, 1])
        enr = sb("enr", [P, 2])
        spot = dst_row[:, :, :].rearrange("q p t -> q (p t)").bitcast(F32)

        def carve(at, n):
            return spot[:, at * W2:(at + n) * W2].rearrange("p (s w) -> p s w", w=W2)

        h0, v, y, yg, xb = carve(0, 2), carve(2, 4), carve(6, 2), carve(8, 4), carve(12, 4)
        cst = sb("cst", [P, 2, 6])
        cmv = sb("cmv", [P, 2, 2, 2])
        cstd = sb("cstd", [P, 2, 2])
        cnr = sb("cnr", [P, 2, 2, 2])

        psT = [ctx.enter_context(nc.psum_tensor(f"psT{i}", [P, W2], F32)) for i in range(2)]
        psM = [ctx.enter_context(nc.psum_tensor(f"psM{i}", [P, W2], F32)) for i in range(NBK)]
        psS = ctx.enter_context(nc.psum_tensor("psS", [P, W2], F32))

        s_w = [sem(f"s_w{l}") for l in range(2)]
        s_bias1 = sem("s_bias1")
        s_pool_go = sem("s_pool_go")
        s_dve_go = sem("s_dve_go")
        s_small = sem("s_small")
        s_edges = sem("s_edges")
        s_dst_row = sem("s_dst_row")
        s_clear = sem("s_clear")
        s_const = sem("s_const")
        s_pool = sem("s_pool")
        s_loop_hi = sem("s_loop_hi")
        s_loop_lo = sem("s_loop_lo")
        s_basis_raw = sem("s_basis_raw")
        s_basis_hi = [sem(f"s_basis_hi{l}") for l in range(2)]
        s_basis_lo = [sem(f"s_basis_lo{l}") for l in range(2)]
        s_td = sem("s_td")
        s_tmax = sem("s_tmax")
        s_exp = sem("s_exp")
        s_dst = sem("s_dst")
        s_dummy = sem("s_dummy")
        s_agg_init = sem("s_agg_init")
        s_agg = sem("s_agg")
        a_x = [sem(f"a_x{i}") for i in range(XS)]
        a_st = sem("a_st")
        a_mv = sem("a_mv")
        a_std = sem("a_std")
        a_rstd = sem("a_rstd")
        a_nmr = sem("a_nmr")
        a_zd = sem("a_zd")
        a_za = sem("a_za")
        a_tr = sem("a_tr")
        a_hi = sem("a_hi")
        a_lo = sem("a_lo")
        a_mm = sem("a_mm")
        a_ev = sem("a_ev")
        a_sum = sem("a_sum")
        a_out = [sem(f"a_out{i}") for i in range(2)]
        names = ["ids", "stat", "mv", "std", "rstd", "nmr", "z", "tr", "hi", "lo", "mm", "cw", "init", "comb",
                 "msg", "mhi", "mlo", "same", "dup", "dupc", "sidx", "smm", "magg", "scat"]
        e = [{n: sem(f"e{l}_{n}") for n in names} for l in range(2)]
        for l in range(2):
            e[l]["row"] = [sem(f"e{l}_row{i}") for i in range(TE)]
            e[l]["coef"] = [sem(f"e{l}_coef{i}") for i in range(TE)]
        c_p = [sem(f"c_p{i}") for i in range(2)]
        c_x = [sem(f"c_x{i}") for i in range(XS)]
        c_a = [sem(f"c_a{i}") for i in range(2)]
        c_out = [sem(f"c_out{i}") for i in range(2)]
        c_tr = sem("c_tr")
        c_hi = sem("c_hi")
        c_lo = sem("c_lo")
        c_mm = sem("c_mm")
        c_h0 = sem("c_h0")
        c_v = sem("c_v")
        c_st = sem("c_st")
        c_mv = sem("c_mv")
        c_std = sem("c_std")
        c_rstd = sem("c_rstd")
        c_nmr = sem("c_nmr")
        c_y = sem("c_y")
        c_yg = sem("c_yg")
        c_xb = sem("c_xb")
        c_o = sem("c_o")

        def after(eng, s, count):
            if not isinstance(count, int) or count > 0:
                eng.wait_ge(s, count)

        def ran(i, n):
            return not isinstance(i, int) or 0 <= i < n

        def looped(eng, first, trips, late, body):
            for it in range(first, 1):
                body(it)
            with eng.Fori(1, trips - late) as it:
                body(it)
            for it in range(trips - late, trips):
                body(it)

        def node_loop(eng, body):
            looped(eng, -1, NQ // TA + 2, 3, body)

        block = ctx.enter_context(nc.Block())

        def flat(v):
            return v.rearrange("(a n) -> a n", a=1)

        whole = "p k n -> p (k n)"

        @block.sync
        def _(sp):
            def load_weights(l, loop_w):
                sp.dma_start(loop_raw[:, l], loop_w.rearrange("(k p) n -> p k n", p=P)).then_inc(s_w[l], 16)

            def load_small():
                sp.dma_start(ctime[:, :], flat(current_time).to_broadcast([P, 1])).then_inc(s_small, 16)
                for j in range(2):
                    sp.dma_start(g_bc[:, j, :], flat(ln_g).to_broadcast([P, D])).then_inc(s_small, 16)
                    sp.dma_start(b_bc[:, j, :], flat(ln_b).to_broadcast([P, D])).then_inc(s_small, 16)

            def load_x(it):
                for k in range(XS):
                    g = XS * it + k
                    if not ran(g, NG):
                        continue
                    after(sp, a_zd, 2 * g - 2 * XS + 2)
                    after(sp, a_za, 2 * g - 2 * XS + 2)
                    sp.dma_start(xg[:, k], rows(x, g)).then_inc(a_x[k], 16)
                    if isinstance(g, int) and g == 0:
                        load_weights(0, loop_w1)
                        for j in range(2):
                            sp.dma_start(bias1_bc[:, j, :], flat(bias1).to_broadcast([P, D])).then_inc(s_bias1, 16)

            def load_lists():
                sp.wait_ge(s_clear, 5)
                for t, v in ((src_i, src), (type_i, edge_type), (dst_i, dst), (etime, edge_time)):
                    sp.dma_start(t[0:FULL, :], v[0:FULL * ET].rearrange("(p t) -> p t", t=ET)).then_inc(s_edges, 16)
                    sp.dma_start(t[FULL:P, 0:REST], flat(v[FULL * ET:E])).then_inc(s_edges, 16)

            def load_agg_init():
                for j in range(TG):
                    sp.dma_start(agg_init[:, j, :], flat(bias2).to_broadcast([P, D])).then_inc(s_agg_init, 16)

            def load_dst_row(part):
                a = bass.ds(part * (E // ROW_PARTS), E // ROW_PARTS)
                sp.dma_start(dst_row[:, :, :].rearrange("q p t -> q (p t)")[:, a],
                             flat(dst)[:, a].to_broadcast([P, E // ROW_PARTS])).then_inc(s_dst_row, 16)

            def load_basis_bank(kh, b):
                sp.dma_start(basis_raw[:, kh, bass.ds(b * W2, W2)],
                             basis1[bass.ds(b * 2, 2), kh * P:(kh + 1) * P, :].rearrange("b p n -> p b n")
                             ).then_inc(s_basis_raw, 16)

            def load_basis2():
                for kh in range(KH):
                    sp.dma_start(basis_raw[:, kh], basis2[:, kh * P:(kh + 1) * P, :].rearrange("b p n -> p b n")
                                 ).then_inc(s_basis_raw, 16)

            load_x(0)
            with sp.Fori(1, 1 + NBK) as it:
                load_x(it)
                load_basis_bank(0, it - 1)
            load_lists()
            with sp.Fori(1 + NBK, 1 + 2 * NBK) as it:
                load_x(it)
                load_basis_bank(1, it - (1 + NBK))
            load_weights(1, loop_w2)
            with sp.Fori(1 + LATE, 1 + LATE + ROW_PARTS) as it:
                load_x(it)
                load_dst_row(it - (1 + LATE))
            load_small()
            with sp.Fori(1 + LATE + ROW_PARTS, NG // XS) as it:
                load_x(it)
            load_x(NG // XS)
            sp.wait_ge(a_sum, NQ)
            sp.dma_start(new_rows(pre1), ag[P - NEW:P, (NG - 1) % 2]).then_inc(a_out[(NG - 1) % 2], 16)

            load_agg_init()
            sp.wait_ge(s_agg_init, 16 * TG)

            with sp.Fori(0, NG - 1) as g:
                sp.wait_ge(e[0]["hi"], g + 1)
                sp.dma_start(rows(agg2, g), agg_init[:, :, :].rearrange("p j d -> p (j d)")).then_inc(s_agg, 16)
            sp.dma_start(new_rows(agg2), agg_init[P - NEW:P, :, :].rearrange("p j d -> p (j d)")).then_inc(s_agg, 16)

            sp.wait_ge(s_basis_hi[0], KH * NBK)
            sp.wait_ge(s_basis_lo[0], KH * NBK)
            load_basis2()

            def load_pre(g, s):
                after(sp, c_tr, 2 * g - 2)
                sp.dma_start(zg[:, s], rows(pre1, g)).then_inc(c_p[s], 16)

            def load_x_again(g, k):
                after(sp, c_xb, 2 * g - 2 * XS + 2)
                after(sp, c_h0, 2 * g - 2 * XS + 2)
                sp.dma_start(xg[:, k], rows(x, g)).then_inc(c_x[k], 16)

            def load_agg(g, s):
                after(sp, c_mm, 2 * g - 2)
                sp.dma_start(ag[:, s], rows(agg2, g)).then_inc(c_a[s], 16)

            def load_c(it):
                for k in range(XS):
                    g = XS * it + k
                    if ran(g, NG):
                        load_pre(g, k % 2)
                        load_x_again(g, k)
                        load_agg(g, k % 2)

            sp.wait_ge(e[0]["scat"], 16 * ET)
            sp.wait_ge(e[1]["hi"], TE)
            for g in range(2):
                load_pre(g, g)
                load_x_again(g, g)
            for g in range(2, XS):
                load_x_again(g, g)
            sp.wait_ge(e[1]["scat"], 16 * ET)
            for g in range(XS):
                load_agg(g, g % 2)
                if g + 2 < XS:
                    load_pre(g + 2, g % 2)
            with sp.Fori(1, NG // XS) as it:
                load_c(it)
            load_c(NG // XS)
            sp.wait_ge(c_out[0], 16 * (NG // 2))
            sp.wait_ge(c_out[1], 16 * (NG // 2))

        @block.gpsimd
        def _(pool):
            pool.memset(ident[:], 0.0).then_inc(s_pool, 1)
            pool.memset(tril[:], 1.0).then_inc(s_pool, 1)
            pool.wait_ge(s_pool, 2)
            pool.affine_select(out=ident[:], in_=ident[:], compare_op=ALU.not_equal, fill=1.0, base=0,
                               pattern=[[-1, P]], channel_multiplier=1).then_inc(s_const, 1)
            pool.affine_select(out=tril[:], in_=tril[:], compare_op=ALU.is_gt, fill=0.0, base=0,
                               pattern=[[-1, P]], channel_multiplier=1).then_inc(s_const, 1)
            pool.memset(eps[:], LN_EPS).then_inc(s_const, 1)
            pool.memset(src_i[:], 0).then_inc(s_clear, 1)
            pool.memset(type_i[:], 0).then_inc(s_clear, 1)
            pool.memset(dst_i[:], N + P - 1).then_inc(s_clear, 1)
            pool.memset(etime[:], 3.0e38).then_inc(s_clear, 1)
            pool.memset(dst_row[:, FULL, :], N + P - 1).then_inc(s_clear, 1)
            pool.memset(zero_row[:], 0.0).then_inc(s_dst, 1)
            pool.iota(spare[:], pattern=[[0, ET]], base=N, channel_multiplier=1,
                      allow_small_or_imprecise_dtypes=True).then_inc(s_dst, 1)
            pool.wait_ge(s_dst, 1)
            for t in (pre1, agg2):
                pool.dma_start(t[N:N + P, :], zero_row[:]).then_inc(s_dummy, 16)

            def nodes_a(it):
                for k in range(TA):
                    q = TA * it + k
                    if ran(q, NQ):
                        h, s = k % 2, k // 2 % 2
                        if h == 0:
                            after(pool, a_out[s], 16 * (2 * it + k // 4))
                        pool.wait_ge(a_ev, q + 1)
                        pool.tensor_tensor(ag[:, s, h * W2:(h + 1) * W2], og[:, s, h * W2:(h + 1) * W2],
                                           bias1_bc[:, :, :].rearrange("p j d -> p (j d)"), ALU.add).then_inc(a_sum, 1)

            pool.wait_ge(s_bias1, 32)
            nodes_a(0)
            with pool.Fori(1, LATE + 1) as it:
                nodes_a(it)
            pool.wait_ge(s_edges, 16 * 8)
            pool.tensor_copy(src_type[:, :, 0], src_i[:]).then_inc(s_pool, 1)
            pool.tensor_copy(src_type[:, :, 1], type_i[:]).then_inc(s_pool, 1)
            pool.wait_ge(s_pool, 4)
            with pool.Fori(LATE + 1, LATE + 1 + KH * NBK) as it:
                nodes_a(it)
                part = bass.ds((it - (LATE + 1)) * W2, W2)
                pool.wait_ge(s_basis_hi[0], it - LATE)
                pool.tensor_tensor(basis_lo[:, :, :].rearrange(whole)[:, part], basis_raw[:, :, :].rearrange(whole)[:, part],
                                   basis_hi[:, :, :].bitcast(F32).rearrange(whole)[:, part], ALU.subtract
                                   ).then_inc(s_basis_lo[0], 1)
            for it in range(LATE + 1 + KH * NBK, NQ // TA - 2):
                nodes_a(it)
            pool.wait_ge(s_td, 3)
            pool.partition_all_reduce(tmax[:, 1:2], tmax[:, 0:1], P, RMAX).then_inc(s_tmax, 1)

            for l in range(2):
                el = e[l]
                table = x if l == 0 else pre1
                comp = comp1 if l == 0 else comp2
                target = pre1 if l == 0 else agg2
                def index(t, s, turn):
                    after(pool, el["row"][s], 16 * turn)
                    after(pool, el["coef"][s], 16 * turn)
                    pool.tensor_copy(ids[:, s], src_type[:, bass.ds(t, 1), :].rearrange("p a b -> p (a b)")
                                     ).then_inc(el["ids"], 1)

                def gather_rows(t, s):
                    pool.wait_ge(el["ids"], t + 1)
                    after(pool, el["tr"], t - TE + 1)
                    pool.sem_inc(s_pool_go, 1)
                    pool.indirect_dma_start(out=xe[:, s], out_offset=None, in_=table[:, :],
                                            in_offset=bass.IndirectOffsetOnAxis(ap=ids[:, s, 0:1], axis=0)
                                            ).then_inc(el["row"][s], 16)

                def gather_coefs(t, s):
                    pool.wait_ge(el["ids"], t + 1)
                    after(pool, el["cw"], t - TE + 1)
                    pool.sem_inc(s_pool_go, 1)
                    pool.indirect_dma_start(out=cr[:, s], out_offset=None, in_=comp[:, :],
                                            in_offset=bass.IndirectOffsetOnAxis(ap=ids[:, s, 1:2], axis=0)
                                            ).then_inc(el["coef"][s], 16)

                def scatter(t, s):
                    after(pool, el["scat"], 16 * t)
                    if l == 0 and isinstance(t, int) and t == 0:
                        pool.wait_ge(a_out[0], 16 * (NG // 2))
                        pool.wait_ge(a_out[1], 16 * (NG // 2))
                    if l == 1 and isinstance(t, int) and t == 0:
                        pool.wait_ge(s_agg, 16 * NG)
                    pool.wait_ge(el["magg"], t + 1)
                    pool.wait_ge(el["sidx"], t + 1)
                    pool.sem_inc(s_pool_go, 1)
                    pool.indirect_dma_start(out=target[:, :],
                                            out_offset=bass.IndirectOffsetOnAxis(ap=sidx[:, s, :], axis=0),
                                            in_=magg[:, s], in_offset=None, compute_op=ALU.add
                                            ).then_inc(el["scat"], 16)

                def edges(it):
                    for k in range(TE):
                        t = TE * it + k
                        if ran(t + 3, ET):
                            index(t + 3, (k + 3) % TE, it + (k + 3) // TE)
                            gather_rows(t + 3, (k + 3) % TE)
                            gather_coefs(t + 3, (k + 3) % TE)
                        if ran(t - 1, ET):
                            scatter(t - 1, (k - 1) % 2)

                if l == 0:
                    for t in range(3):
                        index(t, t, 0)
                        gather_rows(t, t)
                        gather_coefs(t, t)
                        nodes_a(NQ // TA - 2 + t)
                    pool.wait_ge(s_dummy, 32)
                else:
                    pool.wait_ge(e[0]["cw"], ET)
                    pool.wait_ge(e[0]["tr"], ET)
                    for t in range(3):
                        index(t, t, 0)
                        gather_coefs(t, t)
                    pool.wait_ge(e[0]["scat"], 16 * ET)
                    for t in range(3):
                        gather_rows(t, t)
                looped(pool, 0, ET // TE + 1, 2, edges)

            def nodes_c(it):
                for k in range(TA):
                    q = TA * it + k - 3
                    if ran(q, NQ):
                        h = (k - 3) % 2
                        if h == 0:
                            pool.wait_ge(c_x[(k - 3) // 2 % XS], 16 * (it + 1 + (k - 3) // TA))
                        after(pool, c_o, q - 3)
                        pool.tensor_tensor(xb[:, (k - 3) % 4], xg[:, (k - 3) // 2 % XS, h * W2:(h + 1) * W2],
                                           b_bc[:, :, :].rearrange("p j d -> p (j d)"), ALU.add).then_inc(c_xb, 1)
                        pool.wait_ge(c_y, q + 1)
                        pool.tensor_tensor(yg[:, (k - 3) % 4], y[:, h],
                                           g_bc[:, :, :].rearrange("p j d -> p (j d)"), ALU.mult).then_inc(c_yg, 1)

            node_loop(pool, nodes_c)

        @block.tensor
        def _(pe):
            pe.wait_ge(s_const, 3)

            def transposes(bank, tile, done):
                n = tile.shape[1] // P
                for i in range(n):
                    last = pe.transpose(psT[bank][:, i * P:(i + 1) * P], tile[:, i * P:(i + 1) * P], ident[:])
                last.then_inc(done, 1)

            def node_products(layer, b, fresh):
                for j in range(2):
                    o = psM[b][:, j * D:(j + 1) * D]
                    for kh in range(KH):
                        c = (j * KH + kh) * P
                        for h, w in ((hi, loop_hi), (hi, loop_lo), (lo, loop_hi)):
                            last = pe.matmul(o, h[:, b, c:c + P], w[:, layer, kh, :], start=fresh,
                                             stop=(layer == 0 and j == 1 and kh == KH - 1 and h is lo),
                                             skip_group_check=True)
                            fresh = False
                return last

            def nodes_a(it):
                for k in range(TA):
                    q = TA * it + k
                    if ran(q + 1, NQ):
                        pe.wait_ge(a_zd, q + 2)
                        pe.wait_ge(a_za, q + 2)
                        after(pe, a_hi, q)
                        after(pe, a_lo, q)
                        h = (k + 1) % 2
                        transposes(h, zg[:, (k + 1) // 2 % 2, h * W2:(h + 1) * W2], a_tr)
                    if ran(q, NQ):
                        after(pe, a_ev, q - 1)
                        pe.wait_ge(a_hi, q + 1)
                        pe.wait_ge(a_lo, q + 1)
                        if isinstance(q, int) and q == 0:
                            pe.wait_ge(s_loop_hi, 1)
                            pe.wait_ge(s_loop_lo, 1)
                        node_products(0, k % 2, True).then_inc(a_mm, 1)

            def nodes_c(it):
                for k in range(TA):
                    q = TA * it + k
                    if ran(q + 1, NQ):
                        h, s = (k + 1) % 2, (k + 1) // 2 % 2
                        if h == 0:
                            pe.wait_ge(c_p[s], 16 * (2 * it + (k + 1) // 4 + 1))
                        after(pe, c_hi, q)
                        after(pe, c_lo, q)
                        transposes(h, zg[:, s, h * W2:(h + 1) * W2], c_tr)
                    if ran(q, NQ):
                        h, s = k % 2, k // 2 % 2
                        after(pe, c_v, q - 1)
                        pe.wait_ge(c_hi, q + 1)
                        pe.wait_ge(c_lo, q + 1)
                        node_products(1, h, True)
                        if h == 0:
                            pe.wait_ge(c_a[s], 16 * (2 * it + k // 4 + 1))
                        pe.matmul(psM[h][:], ident[:], ag[:, s, h * W2:(h + 1) * W2], start=False, stop=True,
                                  skip_group_check=True).then_inc(c_mm, 1)

            node_loop(pe, nodes_a)

            for l in range(2):
                el = e[l]

                def transpose_edges(t, s, turn):
                    if l == 0:
                        pe.wait_ge(el["z"], t + 1)
                    else:
                        pe.wait_ge(el["row"][s], 16 * (turn + 1))
                    transposes(s % 2, xe[:, s], el["tr"])

                def combine_duplicates(t, s):
                    pe.wait_ge(el["same"], t + 1)
                    pe.wait_ge(el["mhi"], t + 1)
                    after(pe, el["magg"], t)
                    pe.matmul(psS[:, 0:D], same[:, s], msg_hi[:, s], start=True, stop=False)
                    pe.wait_ge(el["mlo"], t + 1)
                    pe.matmul(psS[:, 0:D], same[:, s], msg_lo[:, s], start=False, stop=True).then_inc(el["smm"], 1)

                if l == 1:
                    pe.wait_ge(e[0]["magg"], ET)

                def edges(it):
                    for k in range(TE):
                        t = TE * it + k
                        for b in range(NBK):
                            if ran(t, ET):
                                if isinstance(t, int) and t == 0:
                                    if l == 1:
                                        pe.wait_ge(s_basis_hi[1], b + 1)
                                        pe.wait_ge(s_basis_lo[1], b + 1)
                                    elif b == 0:
                                        pe.wait_ge(s_basis_hi[0], KH * NBK)
                                        pe.wait_ge(s_basis_lo[0], KH * NBK)
                                        pe.wait_ge(a_ev, NQ)
                                if b == 0:
                                    pe.wait_ge(el["hi"], t + 1)
                                    pe.wait_ge(el["lo"], t + 1)
                                    after(pe, el["init"], 2 * t)
                                else:
                                    after(pe, el["comb"], CH * (t - 1) + 2 * b)
                                n = 0
                                for kh in range(KH):
                                    for h, w in ((hi, basis_hi), (hi, basis_lo), (lo, basis_hi)):
                                        last = pe.matmul(psM[b][:], h[:, k % 2, kh * P:(kh + 1) * P],
                                                         w[:, kh, b * W2:(b + 1) * W2], start=(n == 0), stop=(n == 3 * KH - 1))
                                        n += 1
                                last.then_inc(el["mm"], 1)
                            if b == 1 and ran(t + 1, ET):
                                transpose_edges(t + 1, (k + 1) % TE, it + (k + 1) // TE)
                            if b == 3 and ran(t - 1, ET):
                                combine_duplicates(t - 1, (k - 1) % 2)

                looped(pe, -1, ET // TE + 1, 2, edges)

            pe.wait_ge(e[1]["magg"], ET)
            node_loop(pe, nodes_c)

        @block.scalar
        def _(act):
            act.preload_act_table(ACT.Sqrt)

            def split_loop(l):
                act.wait_ge(s_w[l], 16)
                act.activation(loop_hi[:, l], loop_raw[:, l], ACT.Copy).then_inc(s_loop_hi, 1)

            split_loop(0)
            act.wait_ge(s_const, 3)

            def split_hi(s, w, done):
                act.activation(hi[:, s, 0:w], psT[s][:, 0:w], ACT.Relu).then_inc(done, 1)

            def nodes_a(it):
                for k in range(TA):
                    q = TA * it + k
                    if ran(q - 1, NQ):
                        h, s = (k - 1) % 2, (k - 1) // 2 % 2
                        after(act, a_sum, q - 4)
                        act.wait_ge(a_mm, q)
                        act.activation(og[:, s, h * W2:(h + 1) * W2], psM[h][:], ACT.Copy).then_inc(a_ev, 1)
                    if ran(q + 1, NQ):
                        act.wait_ge(a_tr, q + 2)
                        after(act, a_mm, q)
                        split_hi((k + 1) % 2, W2, a_hi)
                    if ran(q + 2, NQ):
                        act.wait_ge(a_nmr, 4 * it + (k + 2) // 2 + 1)
                        after(act, a_tr, q - 1)
                        h, s = k % 2, (k + 2) // 2
                        o = h * W2 + D
                        c = bass.ds(4 * TG * it + TG * s + 2 * h + 1, 1)
                        act.activation(zg[:, s % 2, o:o + D], xg[:, s % XS, o:o + D], ACT.Identity,
                                       bias=nmr[:, c], scale=rstd[:, c]).then_inc(a_za, 1)
                    if k % 2 == 0 and ran(4 * it + k // 2 + 2, NG):
                        g = 4 * it + k // 2 + 2
                        act.wait_ge(a_mv, g + 1)
                        after(act, a_rstd, g - 1)
                        act.activation(std[:, k // 2 % 2], mv[:, k // 2 % 2, :, 1], ACT.Sqrt, bias=eps[:]).then_inc(a_std, 1)
                    if k % 2 == 1 and ran(4 * it + k // 2 - 1, NG - 1):
                        g = 4 * it + k // 2 - 1
                        s = (k // 2 - 1) % 2
                        act.wait_ge(a_sum, 2 * g + 2)
                        act.dma_start(rows(pre1, g), ag[:, s]).then_inc(a_out[s], 16)

            def decay_edges():
                act.wait_ge(s_td, 6)
                act.activation(decay[:], etime[:], ACT.Exp, scale=-RATE).then_inc(s_exp, 1)

            nodes_a(-1)
            nodes_a(0)
            with act.Fori(1, LATE) as it:
                nodes_a(it)
            act.wait_ge(s_basis_raw, 16 * KH * NBK)
            with act.Fori(LATE, LATE + KH * NBK) as it:
                nodes_a(it)
                part = bass.ds((it - LATE) * W2, W2)
                act.activation(basis_hi[:, :, :].rearrange(whole)[:, part], basis_raw[:, :, :].rearrange(whole)[:, part],
                               ACT.Copy).then_inc(s_basis_hi[0], 1)
            with act.Fori(LATE + KH * NBK, NQ // TA - 1) as it:
                nodes_a(it)
            decay_edges()
            act.preload_act_table(ACT.Sqrt)

            def std_e(t):
                act.wait_ge(e[0]["mv"], t + 1)
                act.activation(estd[:], emv[:, 1:2], ACT.Sqrt, bias=eps[:]).then_inc(e[0]["std"], 1)

            std_e(0)
            nodes_a(NQ // TA - 1)
            std_e(1)
            nodes_a(NQ // TA)

            for l in range(2):
                el = e[l]

                def start_e(t, s):
                    act.wait_ge(el["cw"], t + 1)
                    if l == 0 and isinstance(t, int) and t == 0:
                        act.wait_ge(a_out[0], 16 * (NG // 2))
                    after(act, el["msg"], t - 1)
                    act.wait_ge(el["mm"], NBK * t + 1)
                    for j in range(2):
                        act.activation(acc[:, s, j], psM[0][:, j * D:(j + 1) * D], ACT.Copy, scale=cw[:, s, j:j + 1]
                                       ).then_inc(el["init"], 1)

                def hi_e(t, s):
                    act.wait_ge(el["tr"], t + 1)
                    after(act, el["mm"], NBK * (t - 1))
                    split_hi(s, D, el["hi"])

                def magg_e(t, s):
                    act.wait_ge(el["smm"], t + 1)
                    after(act, el["scat"], 16 * (t - 1))
                    act.activation(magg[:, s], psS[:, 0:D], ACT.Copy).then_inc(el["magg"], 1)

                if l == 1:
                    act.wait_ge(s_basis_raw, 16 * (KH * NBK + KH))
                    act.wait_ge(e[0]["mm"], NBK * ET)
                    for b in range(NBK):
                        c = slice(b * W2, (b + 1) * W2)
                        act.activation(basis_hi[:, :, c], basis_raw[:, :, c], ACT.Copy).then_inc(s_basis_hi[1], 1)

                def edges(it):
                    for k in range(TE):
                        t = TE * it + k
                        if ran(t, ET):
                            start_e(t, k % 2)
                        if ran(t - 1, ET):
                            s = (k - 1) % 2
                            act.wait_ge(el["msg"], t)
                            after(act, el["smm"], t - 2)
                            act.activation(msg_hi[:, s], msg[:, s], ACT.Copy).then_inc(el["mhi"], 1)
                        if ran(t + 1, ET):
                            hi_e(t + 1, (k + 1) % 2)
                        if l == 0 and ran(t + 2, ET) and not (isinstance(t, int) and t < 0):
                            std_e(t + 2)
                        if ran(t - 1, ET):
                            magg_e(t - 1, (k - 1) % 2)

                edges(-1)
                if l == 0:
                    split_loop(1)
                looped(act, 0, ET // TE + 1, 2, edges)

            def nodes_c(it):
                for k in range(TA):
                    q = TA * it + k

                    def h0_c(j):
                        a = k % 2 * W2 + j * D
                        c = bass.ds(2 * q + j, 1)
                        return act.activation(h0[:, k % 2, j * D:(j + 1) * D], xg[:, k // 2, a:a + D], ACT.Relu,
                                              bias=nmr[:, c], scale=rstd[:, c])

                    if ran(q + 1, NQ):
                        act.wait_ge(c_tr, q + 2)
                        after(act, c_mm, q)
                        split_hi((k + 1) % 2, W2, c_hi)
                    if ran(q - 2, NQ):
                        act.wait_ge(c_mv, q - 1)
                        after(act, c_rstd, q - 3)
                        act.activation(cstd[:, k % 2], cmv[:, k % 2, :, 1], ACT.Sqrt, bias=eps[:]).then_inc(c_std, 1)
                    if ran(q, NQ):
                        if k % 2 == 0:
                            act.wait_ge(c_x[k // 2], 16 * (it + 1))
                        after(act, c_v, q - 1)
                        h0_c(0)
                        h0_c(1).then_inc(c_h0, 1)
                    if ran(q - 3, NQ):
                        s = (k - 3) % 2
                        act.wait_ge(c_nmr, q - 2)
                        after(act, c_yg, q - 4)
                        for j in range(2):
                            last = act.activation(y[:, s, j * D:(j + 1) * D], v[:, (k - 3) % 4, j * D:(j + 1) * D],
                                                  ACT.Identity, bias=cnr[:, s, 1, j:j + 1], scale=cnr[:, s, 0, j:j + 1])
                        last.then_inc(c_y, 1)
                    if k % 2 == 1 and ran(4 * it + k // 2 - 3, NG):
                        g, s = 4 * it + k // 2 - 3, (k // 2 - 3) % 2
                        act.wait_ge(c_o, 2 * g + 2)
                        if isinstance(g, int) and g == NG - 1:
                            act.dma_start(new_rows(out), og[P - NEW:P, s]).then_inc(c_out[s], 16)
                        else:
                            act.dma_start(rows(out, g), og[:, s]).then_inc(c_out[s], 16)

            node_loop(act, nodes_c)

        @block.vector
        def _(dve):
            def split_loop(l):
                dve.wait_ge(s_loop_hi, l + 1)
                dve.tensor_tensor(loop_lo[:, l], loop_raw[:, l], loop_hi[:, l].bitcast(F32), ALU.subtract).then_inc(s_loop_lo, 1)

            split_loop(0)
            dve.wait_ge(s_const, 3)

            def split_lo(s, w, done):
                dve.scalar_tensor_tensor(out=lo[:, s, 0:w], in0=psT[s][:, 0:w], scalar=0.0, in1=hi[:, s, 0:w].bitcast(F32),
                                         op0=ALU.max, op1=ALU.subtract).then_inc(done, 1)

            def nodes_a(it):
                for k in range(TA):
                    q = TA * it + k
                    g = 4 * it + k // 2 + 2
                    if k % 2 == 1 and ran(g, NG):
                        c = bass.ds(g * TG, TG)
                        dve.wait_ge(a_std, g + 1)
                        dve.reciprocal(rstd[:, c], std[:, k // 2 % 2]).then_inc(a_rstd, 1)
                    if ran(q + 2, NQ):
                        h, s = k % 2, (k + 2) // 2
                        dve.wait_ge(a_nmr, 4 * it + s + 1)
                        after(dve, a_tr, q - 1)
                        o = h * W2
                        cz = bass.ds(4 * TG * it + TG * s + 2 * h, 1)
                        dve.tensor_scalar(zg[:, s % 2, o:o + D], xg[:, s % XS, o:o + D], rstd[:, cz], nmr[:, cz],
                                          ALU.mult, ALU.add).then_inc(a_zd, 1)
                    if k % 2 == 1 and ran(g, NG):
                        dve.wait_ge(a_rstd, g + 1)
                        dve.scalar_tensor_tensor(out=nmr[:, c], in0=mv[:, k // 2 % 2, :, 0], scalar=-1.0, in1=rstd[:, c],
                                                 op0=ALU.mult, op1=ALU.mult).then_inc(a_nmr, 1)
                    if k % 2 == 0 and ran(g, NG):
                        dve.wait_ge(a_st, g + 1)
                        after(dve, a_nmr, g - 1)
                        dve.sem_inc(s_dve_go, 1)
                        for j in range(TG):
                            last = dve.bn_aggr(mv[:, k // 2 % 2, j], st[:, j])
                        last.then_inc(a_mv, 1)
                    if ran(q + 1, NQ):
                        dve.wait_ge(a_hi, q + 2)
                        split_lo((k + 1) % 2, W2, a_lo)
                    g = 4 * it + k // 2 + 3
                    if ran(g, NG):
                        if k % 2 == 0:
                            dve.wait_ge(a_x[(k // 2 + 3) % XS], 16 * (it + 1 + (k // 2 + 3) // XS))
                            after(dve, a_mv, g)
                        for j in range(2 * (k % 2), 2 * (k % 2) + 2):
                            last = dve.bn_stats(st[:, j], xg[:, (k // 2 + 3) % XS, j * D:(j + 1) * D])
                        if k % 2 == 1:
                            last.then_inc(a_st, 1)

            def age_edges():
                dve.wait_ge(s_edges, 16 * 8)
                dve.wait_ge(s_small, 16 * 5)
                dve.tensor_scalar(decay[:], etime[:], -1.0, ctime[:], ALU.mult, ALU.add).then_inc(s_td, 1)
                dve.wait_ge(s_td, 1)
                dve.tensor_scalar(decay[:], decay[:], 0.0, None, ALU.max).then_inc(s_td, 1)
                dve.wait_ge(s_td, 2)
                dve.tensor_reduce(tmax[:, 0:1], decay[:], AX.X, ALU.max).then_inc(s_td, 1)

            def prepare_edges():
                dve.wait_ge(s_tmax, 1)
                dve.tensor_scalar(tmax[:, 2:3], tmax[:, 1:2], 1e-8, None, ALU.add).then_inc(s_td, 1)
                dve.wait_ge(s_td, 4)
                dve.reciprocal(tmax[:, 3:4], tmax[:, 2:3]).then_inc(s_td, 1)
                dve.wait_ge(s_td, 5)
                dve.tensor_scalar(etime[:], decay[:], tmax[:, 3:4], None, ALU.mult).then_inc(s_td, 1)
                dve.wait_ge(s_dst_row, 16 * ROW_PARTS)
                dve.wait_ge(s_dst, 2)
                dve.tensor_copy(dst_f[:], dst_i[:]).then_inc(s_td, 1)
                dve.wait_ge(s_td, 7)
                dve.tensor_tensor(spare[:], spare[:], dst_f[:], ALU.subtract).then_inc(s_td, 1)

            nodes_a(-1)
            nodes_a(0)
            with dve.Fori(1, NQ // TA - 2) as it:
                nodes_a(it)
            age_edges()
            nodes_a(NQ // TA - 2)
            prepare_edges()

            def measure_e(t, s, turn):
                dve.wait_ge(e[0]["row"][s], 16 * (turn + 1))
                after(dve, e[0]["mv"], t)
                dve.bn_stats(est[:], xe[:, s]).then_inc(e[0]["stat"], 1)

            def aggregate_e(t):
                dve.wait_ge(e[0]["stat"], t + 1)
                after(dve, e[0]["nmr"], t)
                dve.sem_inc(s_dve_go, 1)
                dve.bn_aggr(emv[:], est[:]).then_inc(e[0]["mv"], 1)

            def rstd_e(t):
                dve.wait_ge(e[0]["std"], t + 1)
                after(dve, e[0]["z"], t)
                dve.reciprocal(enr[:, 0:1], estd[:]).then_inc(e[0]["rstd"], 1)

            def nmr_e(t):
                dve.wait_ge(e[0]["rstd"], t + 1)
                dve.scalar_tensor_tensor(out=enr[:, 1:2], in0=emv[:, 0:1], scalar=-1.0, in1=enr[:, 0:1],
                                         op0=ALU.mult, op1=ALU.mult).then_inc(e[0]["nmr"], 1)

            def norm_e(t, s):
                dve.wait_ge(e[0]["nmr"], t + 1)
                dve.tensor_scalar(xe[:, s], xe[:, s], enr[:, 0:1], enr[:, 1:2], ALU.mult, ALU.add).then_inc(e[0]["z"], 1)

            measure_e(0, 0, 0)
            aggregate_e(0)
            nodes_a(NQ // TA - 1)
            rstd_e(0)
            nmr_e(0)
            norm_e(0, 0)
            measure_e(1, 1, 0)
            aggregate_e(1)
            nodes_a(NQ // TA)
            rstd_e(1)
            nmr_e(1)
            norm_e(1, 1)
            dve.wait_ge(s_td, 8)
            dve.wait_ge(s_exp, 1)

            for l in range(2):
                el = e[l]

                def lo_e(t, s):
                    dve.wait_ge(el["hi"], t + 1)
                    split_lo(s, D, el["lo"])

                def lo_messages(t, s):
                    dve.wait_ge(el["mhi"], t + 1)
                    dve.tensor_tensor(msg_lo[:, s], msg[:, s], msg_hi[:, s].bitcast(F32), ALU.subtract).then_inc(el["mlo"], 1)

                def weigh(t, s, slot, turn):
                    dve.wait_ge(el["coef"][slot], 16 * (turn + 1))
                    after(dve, el["comb"], CH * (t - 1))
                    after(dve, el["init"], 2 * (t - 1))
                    dve.tensor_scalar(cw[:, s], cr[:, slot], decay[:, bass.ds(t, 1)], None, ALU.mult).then_inc(el["cw"], 1)

                def combine(t, s, b):
                    if b == 1:
                        dve.wait_ge(el["cw"], t + 1)
                    dve.wait_ge(el["mm"], NBK * t + b + 1)
                    for j in range(2):
                        n = 2 * (b - 1) + j
                        if b == 1:
                            dve.wait_ge(el["init"], 2 * t + j + 1)
                        else:
                            dve.wait_ge(el["comb"], CH * t + n - 1)
                        dve.scalar_tensor_tensor(out=acc[:, s, j], in0=psM[b][:, j * D:(j + 1) * D],
                                                 scalar=cw[:, s, n + 2:n + 3], in1=acc[:, s, j],
                                                 op0=ALU.mult, op1=ALU.add).then_inc(el["comb"], 1)

                def same_e(t, s):
                    after(dve, el["smm"], t - 1)
                    dve.tensor_scalar(same[:, s], dst_row[:, :, bass.ds(t, 1)].rearrange("q p t -> q (p t)"),
                                      dst_f[:, bass.ds(t, 1)], None, ALU.is_equal).then_inc(el["same"], 1)

                def count_e(t, s):
                    dve.wait_ge(el["same"], t + 1)
                    after(dve, el["dupc"], t)
                    dve.tensor_tensor_reduce(out=junk[:], in0=same[:, s].bitcast(F32), in1=tril[:], scale=1.0, scalar=0.0,
                                             op0=ALU.mult, op1=ALU.add, accum_out=dup[:, 0:1]).then_inc(el["dup"], 1)

                def detour_e(t):
                    dve.wait_ge(el["dup"], t + 1)
                    after(dve, el["sidx"], t)
                    dve.tensor_scalar(dup[:, 1:2], dup[:, 0:1], 1.0, spare[:, bass.ds(t, 1)], ALU.min, ALU.mult
                                      ).then_inc(el["dupc"], 1)

                def index_e(t, s):
                    dve.wait_ge(el["dupc"], t + 1)
                    after(dve, el["scat"], 16 * (t - 1))
                    dve.tensor_tensor(sidx[:, s], dup[:, 1:2], dst_f[:, bass.ds(t, 1)], ALU.add).then_inc(el["sidx"], 1)

                if l == 1:
                    for b in range(NBK):
                        c = slice(b * W2, (b + 1) * W2)
                        dve.wait_ge(s_basis_hi[1], b + 1)
                        dve.tensor_tensor(basis_lo[:, :, c], basis_raw[:, :, c], basis_hi[:, :, c].bitcast(F32),
                                          ALU.subtract).then_inc(s_basis_lo[1], 1)

                def edges(it):
                    for k in range(TE):
                        t = TE * it + k
                        s = k % 2
                        here, before, next1 = ran(t, ET), ran(t - 1, ET), ran(t + 1, ET)
                        next2 = l == 0 and ran(t + 2, ET) and not (isinstance(t, int) and t < 0)
                        s2 = (k + 2) % TE
                        if here:
                            same_e(t, s)
                            combine(t, s, 1)
                        if before:
                            lo_messages(t - 1, 1 - s)
                        if next2:
                            measure_e(t + 2, s2, it + (k + 2) // TE)
                        if here:
                            count_e(t, s)
                            combine(t, s, 2)
                        if next2:
                            aggregate_e(t + 2)
                        if here:
                            detour_e(t)
                        if next1:
                            lo_e(t + 1, 1 - s)
                        if here:
                            index_e(t, s)
                            combine(t, s, 3)
                        if next2:
                            rstd_e(t + 2)
                        if next1:
                            weigh(t + 1, 1 - s, (k + 1) % TE, it + (k + 1) // TE)
                        if next2:
                            nmr_e(t + 2)
                        if here:
                            combine(t, s, 4)
                        if next2:
                            norm_e(t + 2, s2)
                        if here:
                            if l == 0 and isinstance(t, int) and t == 0:
                                dve.wait_ge(a_out[1], 16 * (NG // 2))
                            dve.wait_ge(el["comb"], CH * (t + 1))
                            after(dve, el["mlo"], t - 1)
                            dve.tensor_tensor(msg[:, s], acc[:, s, 0], acc[:, s, 1], ALU.add).then_inc(el["msg"], 1)

                edges(-1)
                if l == 0:
                    split_loop(1)
                looped(dve, 0, ET // TE + 1, 2, edges)

            def nodes_c(it):
                for k in range(TA):
                    q = TA * it + k
                    if ran(q - 1, NQ):
                        dve.wait_ge(c_h0, q)
                        after(dve, c_y, q - 4)
                        dve.wait_ge(c_mm, q)
                        dve.scalar_tensor_tensor(out=v[:, (k - 1) % 4], in0=psM[(k - 1) % 2][:], scalar=0.0,
                                                 in1=h0[:, (k - 1) % 2], op0=ALU.max, op1=ALU.add).then_inc(c_v, 1)
                    if ran(q + 1, NQ):
                        dve.wait_ge(c_hi, q + 2)
                        split_lo((k + 1) % 2, W2, c_lo)
                    if ran(q - 2, NQ):
                        b = k % 2
                        dve.wait_ge(c_std, q - 1)
                        after(dve, c_y, q - 3)
                        dve.reciprocal(cnr[:, b, 0], cstd[:, b]).then_inc(c_rstd, 1)
                    if ran(q - 1, NQ):
                        dve.wait_ge(c_v, q)
                        after(dve, c_mv, q - 1)
                        for j in range(2):
                            last = dve.bn_stats(cst[:, j], v[:, (k - 1) % 4, j * D:(j + 1) * D])
                        last.then_inc(c_st, 1)
                    if ran(q - 2, NQ):
                        dve.wait_ge(c_rstd, q - 1)
                        dve.scalar_tensor_tensor(out=cnr[:, b, 1], in0=cmv[:, b, :, 0], scalar=-1.0, in1=cnr[:, b, 0],
                                                 op0=ALU.mult, op1=ALU.mult).then_inc(c_nmr, 1)
                    if ran(q - 5, NQ):
                        h, s = (k - 5) % 2, (k - 5) // 2 % 2
                        if h == 0:
                            after(dve, c_out[s], 16 * (2 * it + (k - 5) // 4))
                        dve.wait_ge(c_xb, q - 4)
                        dve.wait_ge(c_yg, q - 4)
                        dve.tensor_tensor(og[:, s, h * W2:(h + 1) * W2], yg[:, (k - 5) % 4], xb[:, (k - 5) % 4],
                                          ALU.add).then_inc(c_o, 1)
                    if ran(q - 1, NQ):
                        dve.wait_ge(c_st, q)
                        after(dve, c_nmr, q - 2)
                        dve.sem_inc(s_dve_go, 1)
                        for j in range(2):
                            last = dve.bn_aggr(cmv[:, (k - 1) % 2, j], cst[:, j])
                        last.then_inc(c_mv, 1)

            node_loop(dve, nodes_c)


_INS = ['x', 'src', 'dst', 'edge_type_240', 'edge_weight', 'L0_gnn_basis1', 'L0_gnn_comp1', 'L0_gnn_loop_w1',
        'L0_gnn_bias1', 'L0_gnn_basis2', 'L0_gnn_comp2', 'L0_gnn_loop_w2', 'L0_gnn_bias2', 'L0_gnn_ln_g',
        'L0_gnn_ln_b', 'L0_gnn_current_time']


def kernel(**inputs):
    import numpy as _np
    import concourse.bacc as _bacc
    from concourse import mybir as _mybir
    from concourse.bass_utils import run_bass_kernel_spmd as _run

    nc = _bacc.Bacc("TRN2", target_bir_lowering=False, num_devices=1)
    arrays, args = {}, []
    for name in _INS:
        a = _np.ascontiguousarray(inputs[name])
        if a.ndim == 0:
            a = a.reshape(1)
        arrays[f"in_{name}_dram"] = a
        args.append(nc.dram_tensor(f"in_{name}_dram", a.shape, _mybir.dt.from_np(a.dtype), kind="ExternalInput").ap())
    shape = inputs['x'].shape
    out = nc.dram_tensor("out_0_dram", shape, _mybir.dt.from_np(_np.dtype('float32')), kind="ExternalOutput").ap()
    rgcn_kernel(nc, *args, out)
    r = _run(nc, [arrays], core_ids=[0])
    return r.results[0]["out_0_dram"]
```
